# Optimizing a Trainium2 kernel written in Bass

```python
import numpy as np
import jax
import jax.numpy as jnp

def _softmax(x, axis=-1):
    return jax.nn.softmax(x, axis=axis)

def _gelu(x):
    return jax.nn.gelu(x, approximate=True)

def _silu(x):
    return jax.nn.silu(x)

def _sigmoid(x):
    return jax.nn.sigmoid(x)

def _layernorm(x, axis=-1, eps=1e-05):
    m = jnp.mean(x, axis=axis, keepdims=True)
    v = jnp.var(x, axis=axis, keepdims=True)
    return (x - m) / jnp.sqrt(v + eps)

def _scatter_add(tgt, idx, src, axis=0):
    return tgt.at[idx].add(src)

def _segment_sum(src, seg, n):
    return jax.ops.segment_sum(src, seg, n)
kernel_name = 'mk_lm_tower_d1_tok_ids512_r4_778e71'

def setup_inputs(seed: int=0):
    np.random.seed(seed)
    _w = jnp.asarray

    def _rec_inputs():
        import jax
        import jax.numpy as jnp
        _rk = jax.random.key(seed)
        x = jax.random.randint(jax.random.fold_in(_rk, 1), (32, 512), 0, 12564, jnp.int32)
        return x
    x = _rec_inputs()

    def _L0_tok_setup():
        import jax, jax.numpy as jnp
        import numpy as np
        VOCAB = 50257
        D = 128
        B, L = (8, 1024)
        key = jax.random.key(seed)
        k1, k2 = jax.random.split(key)
        x = jax.random.randint(k1, (B, L), 0, VOCAB, dtype=jnp.int64)
        idx2vec = jax.random.normal(k2, (VOCAB, D), dtype=jnp.float32)
        return {'x': x, 'idx2vec': idx2vec}
    _L0_tok_all = _L0_tok_setup()
    _L0_tok_in = {k: v for k, v in _L0_tok_all.items() if k in ('idx2vec',)}
    del _L0_tok_all

    def _L0_attn_setup():
        import jax, jax.numpy as jnp
        import numpy as np
        EPS = 1e-05
        H = 1

        def _silu(x):
            return x * jax.nn.sigmoid(x)

        def _causal_dwconv(x, w):
            K = w.shape[1]
            xp = jnp.pad(x, ((0, 0), (K - 1, 0), (0, 0)))
            out = jax.lax.conv_general_dilated(xp.transpose(0, 2, 1), w[:, None, :], (1,), 'VALID', dimension_numbers=('NCH', 'OIH', 'NCH'), feature_group_count=w.shape[0])
            return out.transpose(0, 2, 1)

        def _l2norm(x):
            return x * jax.lax.rsqrt(jnp.sum(x * x, -1, keepdims=True) + 1e-06)

        def _gated_delta_net(x, q_proj_w, k_proj_w, v_proj_w, b_proj_w, a_proj_w, A_log, dt_bias, q_conv_w, k_conv_w, v_conv_w, g_proj_w, o_norm_w, o_proj_w):
            B, T, D = x.shape
            Dh = D // H
            scale = Dh ** (-0.5)
            q = _silu(_causal_dwconv(x @ q_proj_w.T, q_conv_w))
            k = _silu(_causal_dwconv(x @ k_proj_w.T, k_conv_w))
            v = _silu(_causal_dwconv(x @ v_proj_w.T, v_conv_w))
            beta = jax.nn.sigmoid(x @ b_proj_w.T)
            g = -jnp.exp(A_log) * jax.nn.softplus(x @ a_proj_w.T + dt_bias)
            qh = _l2norm(q.reshape(B, T, H, Dh)) * scale
            kh = _l2norm(k.reshape(B, T, H, Dh))
            vh = v.reshape(B, T, H, Dh)
            xs = (jnp.moveaxis(qh, 1, 0), jnp.moveaxis(kh, 1, 0), jnp.moveaxis(vh, 1, 0), jnp.moveaxis(g, 1, 0), jnp.moveaxis(beta, 1, 0))

            def step(S, inp):
                q_t, k_t, v_t, g_t, b_t = inp
                S = S * jnp.exp(g_t)[..., None, None]
                kv = jnp.einsum('bhk,bhkv->bhv', k_t, S)
                dv = (v_t - kv) * b_t[..., None]
                S = S + k_t[..., None] * dv[..., None, :]
                o_t = jnp.einsum('bhk,bhkv->bhv', q_t, S)
                return (S, o_t)
            S0 = jnp.zeros((B, H, Dh, Dh), x.dtype)
            _, o = jax.lax.scan(step, S0, xs)
            o = jnp.moveaxis(o, 0, 1)
            gate = (x @ g_proj_w.T).reshape(B, T, H, Dh)
            o = o * jax.lax.rsqrt(jnp.mean(o * o, -1, keepdims=True) + EPS) * o_norm_w
            o = o * _silu(gate)
            return o.reshape(B, T, D) @ o_proj_w.T
        key = jax.random.key(seed)
        B, T, D, K = (2, 256, 128, 4)
        ks = jax.random.split(key, 12)
        p = lambda k, shape, s=0.02: jax.random.normal(k, shape, jnp.float32) * s
        return {'x': jax.random.normal(ks[0], (B, T, D), jnp.float32), 'q_proj_w': p(ks[1], (D, D)), 'k_proj_w': p(ks[2], (D, D)), 'v_proj_w': p(ks[3], (D, D)), 'b_proj_w': p(ks[4], (H, D)), 'a_proj_w': p(ks[5], (H, D)), 'A_log': jnp.log(jax.random.uniform(ks[6], (H,), jnp.float32, 1.0, 16.0)), 'dt_bias': jnp.full((H,), -4.6, jnp.float32), 'q_conv_w': p(ks[7], (D, K), 0.2), 'k_conv_w': p(ks[8], (D, K), 0.2), 'v_conv_w': p(ks[9], (D, K), 0.2), 'g_proj_w': p(ks[10], (D, D)), 'o_norm_w': jnp.ones((D,), jnp.float32), 'o_proj_w': p(ks[11], (D, D))}
    _L0_attn_all = _L0_attn_setup()
    _L0_attn_in = {k: v for k, v in _L0_attn_all.items() if k in ('q_proj_w', 'k_proj_w', 'v_proj_w', 'b_proj_w', 'a_proj_w', 'A_log', 'dt_bias', 'q_conv_w', 'k_conv_w', 'v_conv_w', 'g_proj_w', 'o_norm_w', 'o_proj_w')}
    del _L0_attn_all

    def _L0_ffn_setup():
        import jax, jax.numpy as jnp
        import numpy as np
        EPS = 1e-06
        SINKHORN_ITERS = 8
        TEMPERATURE = 1.0
        B, N, D = (4, 2048, 128)
        E, OUT = (8, 128)
        H = 1

        def _sinkhorn(logits):
            t = jnp.log(jnp.clip(logits, EPS)) / TEMPERATURE
            for _ in range(SINKHORN_ITERS):
                t = t - jax.nn.logsumexp(t, axis=-2, keepdims=True)
                t = t - jax.nn.logsumexp(t, axis=-1, keepdims=True)
            return jnp.exp(t)
        key = jax.random.key(seed)
        k1, k2, k3 = jax.random.split(key, 3)
        x = jax.random.normal(k1, (B, N, D), dtype=jnp.float32)
        gate_weight = jax.random.normal(k2, (H, D, E), dtype=jnp.float32)
        experts = jax.random.normal(k3, (E, D, OUT), dtype=jnp.float32) * 0.02
        return {'x': x, 'gate_weight': gate_weight, 'experts': experts}
    _L0_ffn_all = _L0_ffn_setup()
    _L0_ffn_in = {k: v for k, v in _L0_ffn_all.items() if k in ('gate_weight', 'experts')}
    del _L0_ffn_all
    return {'x': x, 'L0_tok_idx2vec': _L0_tok_in['idx2vec'], 'L0_attn_q_proj_w': _L0_attn_in['q_proj_w'], 'L0_attn_k_proj_w': _L0_attn_in['k_proj_w'], 'L0_attn_v_proj_w': _L0_attn_in['v_proj_w'], 'L0_attn_b_proj_w': _L0_attn_in['b_proj_w'], 'L0_attn_a_proj_w': _L0_attn_in['a_proj_w'], 'L0_attn_A_log': _L0_attn_in['A_log'], 'L0_attn_dt_bias': _L0_attn_in['dt_bias'], 'L0_attn_q_conv_w': _L0_attn_in['q_conv_w'], 'L0_attn_k_conv_w': _L0_attn_in['k_conv_w'], 'L0_attn_v_conv_w': _L0_attn_in['v_conv_w'], 'L0_attn_g_proj_w': _L0_attn_in['g_proj_w'], 'L0_attn_o_norm_w': _L0_attn_in['o_norm_w'], 'L0_attn_o_proj_w': _L0_attn_in['o_proj_w'], 'L0_ffn_gate_weight': _L0_ffn_in['gate_weight'], 'L0_ffn_experts': _L0_ffn_in['experts']}

def reference(x, L0_tok_idx2vec, L0_attn_q_proj_w, L0_attn_k_proj_w, L0_attn_v_proj_w, L0_attn_b_proj_w, L0_attn_a_proj_w, L0_attn_A_log, L0_attn_dt_bias, L0_attn_q_conv_w, L0_attn_k_conv_w, L0_attn_v_conv_w, L0_attn_g_proj_w, L0_attn_o_norm_w, L0_attn_o_proj_w, L0_ffn_gate_weight, L0_ffn_experts):
    import jax
    import jax.numpy as jnp

    def _L0_tok_ref(x, idx2vec):
        import jax, jax.numpy as jnp
        import numpy as np
        VOCAB = 50257
        D = 128
        B, L = (8, 1024)
        return jnp.take(idx2vec, x, axis=0)

    def _L0_attn_ref(x, q_proj_w, k_proj_w, v_proj_w, b_proj_w, a_proj_w, A_log, dt_bias, q_conv_w, k_conv_w, v_conv_w, g_proj_w, o_norm_w, o_proj_w):
        import jax, jax.numpy as jnp
        import numpy as np
        EPS = 1e-05
        H = 1

        def _silu(x):
            return x * jax.nn.sigmoid(x)

        def _causal_dwconv(x, w):
            K = w.shape[1]
            xp = jnp.pad(x, ((0, 0), (K - 1, 0), (0, 0)))
            out = jax.lax.conv_general_dilated(xp.transpose(0, 2, 1), w[:, None, :], (1,), 'VALID', dimension_numbers=('NCH', 'OIH', 'NCH'), feature_group_count=w.shape[0])
            return out.transpose(0, 2, 1)

        def _l2norm(x):
            return x * jax.lax.rsqrt(jnp.sum(x * x, -1, keepdims=True) + 1e-06)

        def _gated_delta_net(x, q_proj_w, k_proj_w, v_proj_w, b_proj_w, a_proj_w, A_log, dt_bias, q_conv_w, k_conv_w, v_conv_w, g_proj_w, o_norm_w, o_proj_w):
            B, T, D = x.shape
            Dh = D // H
            scale = Dh ** (-0.5)
            q = _silu(_causal_dwconv(x @ q_proj_w.T, q_conv_w))
            k = _silu(_causal_dwconv(x @ k_proj_w.T, k_conv_w))
            v = _silu(_causal_dwconv(x @ v_proj_w.T, v_conv_w))
            beta = jax.nn.sigmoid(x @ b_proj_w.T)
            g = -jnp.exp(A_log) * jax.nn.softplus(x @ a_proj_w.T + dt_bias)
            qh = _l2norm(q.reshape(B, T, H, Dh)) * scale
            kh = _l2norm(k.reshape(B, T, H, Dh))
            vh = v.reshape(B, T, H, Dh)
            xs = (jnp.moveaxis(qh, 1, 0), jnp.moveaxis(kh, 1, 0), jnp.moveaxis(vh, 1, 0), jnp.moveaxis(g, 1, 0), jnp.moveaxis(beta, 1, 0))

            def step(S, inp):
                q_t, k_t, v_t, g_t, b_t = inp
                S = S * jnp.exp(g_t)[..., None, None]
                kv = jnp.einsum('bhk,bhkv->bhv', k_t, S)
                dv = (v_t - kv) * b_t[..., None]
                S = S + k_t[..., None] * dv[..., None, :]
                o_t = jnp.einsum('bhk,bhkv->bhv', q_t, S)
                return (S, o_t)
            S0 = jnp.zeros((B, H, Dh, Dh), x.dtype)
            _, o = jax.lax.scan(step, S0, xs)
            o = jnp.moveaxis(o, 0, 1)
            gate = (x @ g_proj_w.T).reshape(B, T, H, Dh)
            o = o * jax.lax.rsqrt(jnp.mean(o * o, -1, keepdims=True) + EPS) * o_norm_w
            o = o * _silu(gate)
            return o.reshape(B, T, D) @ o_proj_w.T
        return _gated_delta_net(x, q_proj_w, k_proj_w, v_proj_w, b_proj_w, a_proj_w, A_log, dt_bias, q_conv_w, k_conv_w, v_conv_w, g_proj_w, o_norm_w, o_proj_w)

    def _L0_ffn_ref(x, gate_weight, experts):
        import jax, jax.numpy as jnp
        import numpy as np
        EPS = 1e-06
        SINKHORN_ITERS = 8
        TEMPERATURE = 1.0
        B, N, D = (4, 2048, 128)
        E, OUT = (8, 128)
        H = 1

        def _sinkhorn(logits):
            t = jnp.log(jnp.clip(logits, EPS)) / TEMPERATURE
            for _ in range(SINKHORN_ITERS):
                t = t - jax.nn.logsumexp(t, axis=-2, keepdims=True)
                t = t - jax.nn.logsumexp(t, axis=-1, keepdims=True)
            return jnp.exp(t)
        b, n, d = x.shape
        e = experts.shape[0]
        m = n // e
        xh = x[:, None, :, :]
        gate_logits = jnp.einsum('bhnd,hde->bhne', xh, gate_weight)
        gates = _sinkhorn(gate_logits)
        g_t = jnp.swapaxes(gates, -1, -2)
        vals, idx = jax.lax.top_k(g_t, m)
        gate_values = jnp.transpose(vals, (2, 0, 1, 3))[..., None]
        routed = jnp.take_along_axis(xh[:, :, None, :, :], idx[..., None], axis=3)
        routed = jnp.transpose(routed, (2, 0, 1, 3, 4))
        expert_w = experts[:, None, :, :]
        outputs = jnp.einsum('ebhmi,ehio->ebhmo', routed, expert_w)
        outputs = outputs * gate_values
        bh_idx = idx.reshape(b, 1, e * m)
        bh_vals = jnp.transpose(outputs, (1, 2, 0, 3, 4)).reshape(b, 1, e * m, outputs.shape[-1])

        def scat(i1, v1):
            return jnp.zeros((n, v1.shape[-1]), dtype=v1.dtype).at[i1].set(v1)
        routed_back = jax.vmap(jax.vmap(scat))(bh_idx, bh_vals)
        return routed_back[:, 0]
    h = _L0_tok_ref(x, L0_tok_idx2vec)
    h = h + _L0_attn_ref(_layernorm(h, axis=-1), L0_attn_q_proj_w, L0_attn_k_proj_w, L0_attn_v_proj_w, L0_attn_b_proj_w, L0_attn_a_proj_w, L0_attn_A_log, L0_attn_dt_bias, L0_attn_q_conv_w, L0_attn_k_conv_w, L0_attn_v_conv_w, L0_attn_g_proj_w, L0_attn_o_norm_w, L0_attn_o_proj_w)
    h = h + _L0_ffn_ref(_layernorm(h, axis=-1), L0_ffn_gate_weight, L0_ffn_experts)
    return h

_drawn_inputs = setup_inputs


def setup_inputs(seed=0):
    import zlib

    import numpy as np

    out = dict(_drawn_inputs(seed))
    spreads = {'L0_attn_o_norm_w': (1.0, 0.6)}
    factors = {'L0_attn_q_proj_w': 8.0,
     'L0_attn_k_proj_w': 8.0,
     'L0_attn_v_proj_w': 8.0,
     'L0_attn_b_proj_w': 8.0,
     'L0_attn_a_proj_w': 8.0,
     'L0_attn_q_conv_w': 8.0,
     'L0_attn_k_conv_w': 8.0,
     'L0_attn_v_conv_w': 8.0,
     'L0_attn_g_proj_w': 8.0,
     'L0_attn_o_proj_w': 8.0}
    for name, (base, spread) in spreads.items():
        noise = np.random.default_rng([zlib.crc32(name.encode()), seed]).standard_normal(out[name].shape)
        drawn = base * np.exp(spread * noise) if base else spread * noise
        out[name] = jnp.asarray(drawn.astype(out[name].dtype))
    for name, factor in factors.items():
        out[name] = (out[name] * factor).astype(out[name].dtype)
    return out
```

```python
from contextlib import ExitStack

import concourse.bass as bass
import numpy as np
from concourse import mybir

SEQS, TOKENS, D = 32, 512, 128
VOCAB = 50257
CHUNK = 128
NC = TOKENS // CHUNK
EXPERTS = 8
TOP = TOKENS // EXPERTS
TAPS = 4
SINKHORN = 8
HALF = 128 // EXPERTS
LEVELS = (2, 4, 8, 16, 32, 64)
RING = 4
SLOTS = 13
STAGES = 5
PE_BANK = 512

W_Q, W_K, W_V, W_G, W_O = (D * i for i in range(5))
W_AB = 5 * D
W_CONV = W_AB + 2
W_NORM = W_CONV + 3 * TAPS
W_ALOG = W_NORM + 1
W_DT = W_ALOG + 1
W_GATE = W_DT + 1
W_EXP = W_GATE + EXPERTS
W_COLS = W_EXP + EXPERTS * D
C_ID, C_TRI, C_NEG, C_BLOCK, C_HIGHER, C_PAIR, C_LEVEL = (D * i for i in range(7))
C_COLS = C_LEVEL + len(LEVELS) * D


def shape_constants():
    r = np.arange(D)
    row, col = r[:, None], r[None, :]

    def doubling(w):
        same = row // (2 * w) == col // (2 * w)
        return np.eye(D) - (same & (row // w % 2 == 1) & (col // w % 2 == 0))

    blocks = [
        np.eye(D),
        row <= col,
        np.where(row <= col, 0.0, -1e30),
        row // EXPERTS == col // EXPERTS,
        (row // EXPERTS == col // EXPERTS) & (row > col),
        doubling(1).T,
    ] + [doubling(w) for w in LEVELS]
    return np.concatenate([b.astype(np.float32) for b in blocks], axis=1)


def tower(nc, ids_d, table_d, weights_d, consts_d, out_d, x2_d, h2_d, logit_d):
    F32 = mybir.dt.float32
    I32 = mybir.dt.int32
    ALU = mybir.AluOpType
    ACT = mybir.ActivationFunctionType
    AX = mybir.AxisListType

    ctx = ExitStack()
    with ctx:
        def sb(name, shape, dt=F32):
            return ctx.enter_context(nc.sbuf_tensor(name, shape, dt))

        def sem(name):
            return ctx.enter_context(nc.semaphore(name))

        w = sb("w", [D, W_COLS])
        cst = sb("cst", [D, C_COLS])
        ids = sb("ids", [D, SEQS * NC], I32)
        wo = sb("wo", [D, D])
        neg_a = sb("neg_a", [D, 1])
        ident = cst[:, C_ID:C_ID + D]
        tri = cst[:, C_TRI:C_TRI + D]
        ones = cst[:, C_TRI + D - 1:C_TRI + D]
        below = cst[:, C_NEG:C_NEG + D]
        idx = sb("idx", [D, 2, NC], I32)
        h_in = sb("h_in", [D, RING, NC, D])
        st1 = sb("st1", [D, NC, 6])
        mv1 = sb("mv1", [D, NC, 2])
        ve1 = sb("ve1", [D, NC])
        rs1 = sb("rs1", [D, NC])
        xn = sb("xn", [D, NC, D])
        xT = sb("xT", [D, TOKENS])
        conv = {s: sb("conv_" + s, [D, TOKENS]) for s in "qkv"}
        qT = sb("qT", [D, TOKENS])
        kT = sb("kT", [D, RING, TOKENS])
        vT = sb("vT", [D, TOKENS])
        gate = sb("gate", [D, RING, NC, D])
        sq = {s: sb("sq_" + s, [D, TOKENS]) for s in "qk"}
        ab = sb("ab", [D, 2, NC])
        z = sb("z", [D, NC])
        zabs = sb("zabs", [D, NC])
        eb = sb("eb", [D, NC])
        ez = sb("ez", [D, NC])
        lz = sb("lz", [D, NC])
        beta = sb("beta", [D, NC])
        beta1 = sb("beta1", [D, NC])
        sp = sb("sp", [D, NC])
        g = sb("g", [D, NC])
        G = sb("G", [D, NC])
        ss = sb("ss", [D, 2, NC])
        rss = sb("rss", [D, 2, NC])
        minus_half = sb("minus_half", [D, 2, NC])
        rk = sb("rk", [D, NC])
        cj = sb("cj", [D, NC])
        knorm = sb("knorm", [D, NC])
        rq = sb("rq", [D, RING, NC])
        gdiff = sb("gdiff", [D, NC])
        gexp = sb("gexp", [D, NC])
        kdec = sb("kdec", [D, NC])
        earg = sb("earg", [D, NC, D])
        E = sb("E", [D, NC, D])
        gam = sb("gam", [D, NC, D])
        gam_tok = sb("gam_tok", [D, RING, NC])
        gam_end = sb("gam_end", [D, RING, NC])
        qg = sb("qg", [D, RING, TOKENS])
        PT = sb("PT", [D, RING, NC, D])
        Kd = sb("Kd", [D, RING, NC, D])
        Vn = sb("Vn", [D, RING, NC, D])
        Braw = sb("Braw", [D, NC, D])
        Bt = sb("Bt", [D, 2, NC, D])
        R0 = sb("R0", [D, 2, NC, D])
        Rl = sb("Rl", [D, 2, NC, D])
        Rf = sb("Rf", [D, 2, NC, D])
        T = sb("T", [D, NC, D])
        Ym = sb("Ym", [D, NC, D])
        S = sb("S", [D, D])
        W = sb("W", [D, D])
        U = sb("U", [D, D])
        O = sb("O", [D, 2, NC, D])
        junk = sb("junk", [D, NC, D])
        so = sb("so", [D, NC])
        rq2 = sb("rq2", [D, NC])
        ms = sb("ms", [D, NC])
        ms1 = sb("ms1", [D, NC])
        rstd = sb("rstd", [D, NC])
        fo = sb("fo", [D, NC])
        on = sb("on", [D, NC, D])
        onT = sb("onT", [D, TOKENS])
        st2 = sb("st2", [D, NC, 6])
        mv2 = sb("mv2", [D, NC, 2])
        ve2 = sb("ve2", [D, NC])
        rs2 = sb("rs2", [D, NC])
        h2 = sb("h2", [D, 2, NC, D])
        x2 = sb("x2", [D, NC, D])
        x2T = sb("x2T", [D, 2, TOKENS])
        lg = sb("lg", [EXPERTS, 2, TOKENS])
        K2 = Rl[:, :, :, :].rearrange("p a c d -> p a (c d)")
        r2 = Bt[:, :, :, :].rearrange("p a c d -> p a (c d)")
        gates2 = R0[:, :, :, :].rearrange("p a c d -> p a (c d)")
        work2 = Rf[:, :, :, :].rearrange("p a c d -> p a (c d)")
        prod2 = O[:, :, :, :].rearrange("p a c d -> p a (c d)")
        blockc = gam[:, 0:2, :]
        col2 = sb("col2", [D, 2, 4])
        top8 = sb("top8", [D, 2, 8])
        wt = sb("wt", [D, SEQS, NC, EXPERTS])
        gcur = sb("gcur", [D, 2, NC, EXPERTS])
        xb = kT[:, 0:2, :]
        hb = gate[:, 0:2, :, :]
        acc = PT[:, 0:2, :, :]
        part = Kd[:, :, :, :]
        sums = Vn[:, 0:3, :, :]
        ob = qg[:, 0:2, :].rearrange("p a (c d) -> p a c d", d=D)

        bank = [ctx.enter_context(nc.psum_tensor(f"bank{i}", [D, PE_BANK], F32)) for i in range(8)]
        PA = bank[0:2]
        PR, PT_, PM = bank[2:5]
        PY = PT_
        CW, CO, PD = bank[5:8]
        KS, US, SS = CW[:, 0:D], CW[:, D:2 * D], CW[:, 2 * D:3 * D]
        SS_P = PM[:, 16:16 + 2 * NC].rearrange("p (a c) -> p a c", c=NC)
        AB_P = PM[:, 0:2 * NC]
        G_P = PM[:, 32:32 + NC]

        def chunks(ap):
            return ap.rearrange("p (c d) -> p c d", d=D)

        ids_in, w_in, cst_in = sem("ids_in"), sem("w_in"), sem("cst_in")
        half_ready = sem("half_ready")
        passed = sem("passed")
        wo_ready, a_exp, neg_a_ready = sem("wo_ready"), sem("a_exp"), sem("neg_a_ready")
        idx_ready = sem("idx_ready")
        gathered = [sem(f"gathered{i}") for i in range(RING)]
        names = """ln_stats ln_aggr ln_var ln_rstd xn_ready x_tp xT_ready gate_p ab_p ab_sb
            gate_ready sums_p beta_e z_ready zabs_ready z_exp z_log beta_one beta_ready soft_ready
            g_ready G_p Gbc_p G_ready ss_ready rss_ready rk_ready cj_ready knorm_ready
            gdiff_ready gexp_ready kdec_ready earg_ready E_ready gam_ready gam_tok_ready
            qg_ready kk_p kq_p braw_ready bt_ready PT_ready r0_ready ktm_p vtm_p kd_ready vn_ready
            t0_p O_ready o_sq rq2_ready ms_ready ms1_ready rstd_ready fo_ready on_ready on_tp onT_ready
            oproj_p h2_ready ln2_stats ln2_aggr ln2_var ln2_rstd x2_ready x2_tp x2T_ready logit_p lg_ready""".split()
        s = {n: sem(n) for n in names}
        proj_p = {t: sem(f"proj_{t}") for t in "qkv"}
        tap = {t: [sem(f"tap_{t}{i}") for i in range(TAPS)] for t in "qkv"}
        silu = {t: sem(f"silu_{t}") for t in "qkv"}
        squared = {t: sem(f"squared_{t}") for t in "qk"}
        y_p, ym_ready, inv_p, r_ready, t_ready = (sem(x) for x in ("y_p", "ym_ready", "inv_p", "r_ready", "t_ready"))
        t0_ready = sem("t0_ready")
        ks_p, w_ready, u_p, u_ready, s_p, s_ready = (
            sem(x) for x in ("ks_p", "w_ready", "u_p", "u_ready", "s_p", "s_ready"))
        x2_stored = [sem(f"x2_stored{i}") for i in range(2)]
        h2_stored = [sem(f"h2_stored{i}") for i in range(2)]
        lg_stored = [sem(f"lg_stored{i}") for i in range(2)]
        k_in = [sem(f"k_in{h}") for h in range(2)]
        sk = [sem(f"sinkhorn{h}") for h in range(2)]
        rows_p = [sem(f"rows_p{h}") for h in range(2)]
        higher_p = [sem(f"higher_p{h}") for h in range(2)]
        wt_p = [sem(f"wt_p{h}") for h in range(2)]
        wt_ready = sem("wt_ready")
        batch_in = [sem(f"batch_in{i}") for i in range(2)]
        gcur_ready = sem("gcur_ready")
        y_chunk = sem("y_chunk")
        part_ready = sem("part_ready")
        acc_e = [sem(f"acc_e{e}") for e in range(4)]
        sum_ab, sum_c = sem("sum_ab"), sem("sum_c")
        out_ready = sem("out_ready")
        out_stored = [sem(f"out_stored{i}") for i in range(2)]

        def stages(i, u):
            found = []
            for k in range(STAGES):
                q = (u - k) % RING
                j = i + (u - k - q) // RING
                n = j * RING + q
                found.append((n, q, j) if not isinstance(n, int) or 0 <= n < SEQS else None)
            return found

        def pipeline(engine, iteration):
            for u in range(2 * RING):
                iteration(*stages(u // RING, u % RING))
            with engine.Fori(2, SEQS // RING) as i:
                for u in range(RING):
                    iteration(*stages(i, u))
            for u in range(RING):
                iteration(*stages(SEQS // RING, u))

        block = ctx.enter_context(nc.Block())

        @block.sync
        def _(sp_):
            sp_.dma_start(ids[:, :], ids_d).then_inc(ids_in, 16)
            sp_.dma_start(w[:, :], weights_d).then_inc(w_in, 16)
            sp_.dma_start(cst[:, :], consts_d).then_inc(cst_in, 16)

            def iteration(gather, project, invert, scan, finish):
                if finish:
                    n, q, j = finish
                    p = q % 2
                    sp_.wait_ge(s["h2_ready"], n + 1)
                    sp_.dma_start(h2_d[bass.ds(n, 1)].rearrange("a p x -> (a p) x"),
                                  h2[:, p].rearrange("p c d -> p (c d)")).then_inc(h2_stored[p], 16)
                    sp_.wait_ge(s["x2T_ready"], n + 1)
                    sp_.dma_start(x2_d[bass.ds(n, 1)].rearrange("a p x -> (a p) x"), x2T[:, p]).then_inc(x2_stored[p], 16)
                    sp_.wait_ge(s["lg_ready"], n + 1)
                    sp_.dma_start(logit_d[bass.ds(n * EXPERTS, EXPERTS)], lg[:, p]).then_inc(lg_stored[p], 16)

            pipeline(sp_, iteration)
            for i in range(2):
                sp_.wait_ge(h2_stored[i], 16 * (SEQS // 2))
                sp_.wait_ge(x2_stored[i], 16 * (SEQS // 2))
                sp_.wait_ge(lg_stored[i], 16 * (SEQS // 2))
            for h in range(2):
                sp_.dma_start(K2[:, h], logit_d[D * h:D * h + D]).then_inc(k_in[h], 16)

            def load(n, p):
                sp_.dma_start(xb[:, p], x2_d[bass.ds(n, 1)].rearrange("a p x -> (a p) x")).then_inc(batch_in[p], 16)
                sp_.dma_start(hb[:, p].rearrange("p c d -> p (c d)"),
                              h2_d[bass.ds(n, 1)].rearrange("a p x -> (a p) x")).then_inc(batch_in[p], 16)

            def store(n, p):
                sp_.wait_ge(out_ready, n + 1)
                sp_.dma_start(out_d[bass.ds(n, 1)].rearrange("a (c p) d -> p (a c) d", p=CHUNK),
                              ob[:, p]).then_inc(out_stored[p], 16)

            load(0, 0)
            load(1, 1)
            with sp_.Fori(0, SEQS // 2 - 1) as i:
                for p in range(2):
                    n = i * 2 + p
                    store(n, p)
                    load(n + 2, p)
            for p in range(2):
                store(SEQS - 2 + p, p)
            for p in range(2):
                sp_.wait_ge(out_stored[p], 16 * (SEQS // 2))

        @block.gpsimd
        def _(pool):
            pool.memset(minus_half[:, :, :], -0.5).then_inc(half_ready, 1)
            pool.wait_ge(half_ready, 1)
            pool.wait_ge(ids_in, 16)
            pool.wait_ge(cst_in, 16)

            def inverse_root(dst, src, n, src_ready, dst_ready):
                pool.wait_ge(src_ready, n + 1)
                pool.tensor_tensor(dst, src, minus_half[:, 0] if len(dst.shape) == 2 else minus_half[:, :, :],
                                   ALU.pow).then_inc(dst_ready, 1)

            def rows(n, q, j):
                if isinstance(n, int) and n < RING:
                    pass
                else:
                    pool.wait_ge(s["h2_ready"], n - RING + 1)
                    pool.sem_inc(passed, 1)
                pool.tensor_copy(idx[:, q % 2], ids[:, bass.ds(n * NC, NC)]).then_inc(idx_ready, 1)
                pool.wait_ge(idx_ready, n + 1)
                pool.sem_inc(passed, 1)
                for c in range(NC):
                    pool.indirect_dma_start(out=h_in[:, q, c, :], out_offset=None, in_=table_d,
                                            in_offset=bass.IndirectOffsetOnAxis(ap=idx[:, q % 2, c:c + 1], axis=0)
                                            ).then_inc(gathered[q], 16)

            def iteration(gather, project, invert, scan, finish):
                if project:
                    inverse_root(rs1[:, :], ve1[:, :], project[0], s["ln_var"], s["ln_rstd"])
                if finish:
                    inverse_root(rstd[:, :], ms1[:, :], finish[0], s["ms1_ready"], s["rstd_ready"])
                if project:
                    n, q, j = project
                    for t, src in (("q", qT[:, :]), ("k", kT[:, q])):
                        pool.wait_ge(silu[t], n + 1)
                        pool.tensor_tensor(sq[t][:, :], src, src, ALU.mult).then_inc(squared[t], 1)
                if finish:
                    inverse_root(rs2[:, :], ve2[:, :], finish[0], s["ln2_var"], s["ln2_rstd"])
                if project:
                    inverse_root(rss[:, :, :], ss[:, :, :], project[0], s["ss_ready"], s["rss_ready"])
                if gather:
                    rows(*gather)
                if project:
                    n, q, j = project
                    pool.wait_ge(s["gam_ready"], n + 1)
                    pool.tensor_tensor(qg[:, q], qT[:, :], gam[:, :, :].rearrange("p c d -> p (c d)"),
                                       ALU.mult).then_inc(s["qg_ready"], 1)
                    pool.wait_ge(s["braw_ready"], n + 1)
                    pool.sem_inc(passed, 1)
                    pool.affine_select(out=Bt[:, q % 2], in_=Braw[:, :, :], compare_op=ALU.not_equal, fill=1.0,
                                       base=0, pattern=[[0, NC], [-1, D]],
                                       channel_multiplier=1).then_inc(s["bt_ready"], 1)
                    pool.wait_ge(s["bt_ready"], n + 1)
                    pool.tensor_tensor(R0[:, q % 2], Bt[:, q % 2],
                                       cst[:, C_PAIR:C_PAIR + D].unsqueeze(1).broadcast_to([D, NC, D]),
                                       ALU.mult).then_inc(s["r0_ready"], 1)

            pipeline(pool, iteration)

            def add(n, p):
                if not (isinstance(n, int) and n == 0):
                    pool.wait_ge(out_ready, n)
                pool.wait_ge(part_ready, n * 2 + 2)
                pool.tensor_tensor(sums[:, 0], part[:, 0], part[:, 1], ALU.add)
                pool.tensor_tensor(sums[:, 1], part[:, 2], part[:, 3], ALU.add).then_inc(sum_ab, 1)
                pool.wait_ge(sum_ab, n + 1)
                pool.tensor_tensor(sums[:, 2], sums[:, 0], sums[:, 1], ALU.add).then_inc(sum_c, 1)

            add(0, 0)
            add(1, 1)
            with pool.Fori(1, SEQS // 2) as i:
                for p in range(2):
                    add(i * 2 + p, p)

        @block.tensor
        def _(pe):
            pe.wait_ge(w_in, 16)
            pe.wait_ge(cst_in, 16)

            def wait_prior(name, n):
                if not (isinstance(n, int) and n == 0):
                    pe.wait_ge(s[name], n)

            def project_part(slot, n, q, j):
                def cols(c):
                    return slice(c * D, c * D + D)

                if slot == 0:
                    pe.wait_ge(s["xn_ready"], n + 1)
                    wait_prior("kd_ready", n)
                    for c in range(NC):
                        mm = pe.transpose(PA[0][:, cols(c)], xn[:, c, :], ident)
                    mm.then_inc(s["x_tp"], 1)
                if slot == 1:
                    pe.wait_ge(s["xT_ready"], n + 1)
                    wait_prior("vn_ready", n)
                    pe.matmul(PA[1][:, :], w[:, W_Q:W_Q + D], xT[:, :], start=True, stop=True).then_inc(proj_p["q"], 1)
                if slot == 2:
                    pe.matmul(PA[0][:, :], w[:, W_K:W_K + D], xT[:, :], start=True, stop=True).then_inc(proj_p["k"], 1)
                if slot == 3:
                    pe.wait_ge(tap["q"][TAPS - 1], n + 1)
                    pe.matmul(PA[1][:, :], w[:, W_V:W_V + D], xT[:, :], start=True, stop=True).then_inc(proj_p["v"], 1)
                if slot == 4:
                    pe.wait_ge(tap["k"][TAPS - 1], n + 1)
                    wait_prior("G_ready", n)
                    for c in range(NC):
                        mm = pe.matmul(AB_P[:, 2 * c:2 * c + 2], xT[:, cols(c)], w[:, W_AB:W_AB + 2], start=True, stop=True)
                    mm.then_inc(s["ab_p"], 1)
                    for c in range(NC):
                        mm = pe.matmul(PA[0][:, cols(c)], xT[:, cols(c)], w[:, W_G:W_G + D], start=True, stop=True)
                    mm.then_inc(s["gate_p"], 1)
                if slot == 6:
                    pe.wait_ge(s["ab_sb"], n + 1)
                    pe.wait_ge(squared["q"], n + 1)
                    for c in range(NC):
                        pe.matmul(SS_P[:, 0, c:c + 1], sq["q"][:, cols(c)], ones, start=True, stop=True)
                    pe.wait_ge(squared["k"], n + 1)
                    for c in range(NC):
                        mm = pe.matmul(SS_P[:, 1, c:c + 1], sq["k"][:, cols(c)], ones, start=True, stop=True)
                    mm.then_inc(s["sums_p"], 1)
                if slot == 7:
                    pe.wait_ge(s["g_ready"], n + 1)
                    pe.wait_ge(s["ss_ready"], n + 1)
                    pe.matmul(G_P, tri, g[:, :], start=True, stop=True).then_inc(s["G_p"], 1)
                    pe.wait_ge(tap["v"][TAPS - 1], n + 1)
                    for c in range(NC):
                        mm = pe.matmul(PA[1][:, cols(c)], g[:, c:c + 1].broadcast_to([D, D]), tri, start=True, stop=True)
                    mm.then_inc(s["Gbc_p"], 1)
                if slot == 8:
                    pe.wait_ge(s["gate_ready"], n + 1)
                    for c in range(NC):
                        mm = pe.matmul(PA[0][:, cols(c)], kT[:, q, cols(c)], kT[:, q, cols(c)], start=True, stop=True)
                    mm.then_inc(s["kk_p"], 1)
                if slot == 9:
                    pe.wait_ge(s["gam_ready"], n + 1)
                    for c in range(NC):
                        mm = pe.matmul(PA[1][:, cols(c)], kT[:, q, cols(c)], qT[:, cols(c)], start=True, stop=True)
                    mm.then_inc(s["kq_p"], 1)
                if slot == 11:
                    pe.wait_ge(s["braw_ready"], n + 1)
                    for c in range(NC):
                        mm = pe.transpose(PA[0][:, cols(c)], kT[:, q, cols(c)], ident)
                    mm.then_inc(s["ktm_p"], 1)
                if slot == 12:
                    pe.wait_ge(s["PT_ready"], n + 1)
                    for c in range(NC):
                        mm = pe.transpose(PA[1][:, cols(c)], vT[:, cols(c)], ident)
                    mm.then_inc(s["vtm_p"], 1)

            def invert_part(slot, n, q, j):
                L = len(LEVELS)
                if slot == 0:
                    pe.wait_ge(s["r0_ready"], n + 1)
                    for c in range(NC):
                        mm = pe.transpose(PT_[:, c * D:c * D + D], R0[:, q % 2, c], ident)
                    mm.then_inc(s["t0_p"], 1)
                elif slot % 2 == 1:
                    l = slot // 2
                    if l == 0:
                        pe.wait_ge(t0_ready, n + 1)
                    else:
                        pe.wait_ge(t_ready, n * (L - 1) + l)
                    for c in range(NC):
                        mm = pe.matmul(PY[:, c * D:c * D + D], Bt[:, q % 2, c], T[:, c], start=True, stop=True)
                    mm.then_inc(y_p, 1)
                else:
                    l = slot // 2 - 1
                    if l:
                        pe.wait_ge(r_ready, n * L + l)
                    elif not (isinstance(n, int) and n == 0):
                        pe.wait_ge(r_ready, n * L)
                    pe.wait_ge(ym_ready, n * L + l + 1)
                    R = R0[:, q % 2] if l == 0 else Rl[:, (l - 1) % 2]
                    for c in range(NC):
                        mm = pe.matmul(PR[:, c * D:c * D + D], Ym[:, c], R[:, c], start=True, stop=True)
                        if l < L - 1:
                            mm = pe.matmul(PT_[:, c * D:c * D + D], R[:, c], Ym[:, c], start=True, stop=True)
                    mm.then_inc(inv_p, 1)

            def scan_part(slot, n, q, j):
                if slot >= 3 * NC:
                    return
                c, phase = divmod(slot, 3)
                o = CO[:, c * D:c * D + D]
                tok = slice(c * D, c * D + D)
                if phase == 0 and c:
                    pe.wait_ge(s_ready, n * (NC - 1) + c)
                    pe.matmul(KS, kT[:, q, tok], S[:, :], start=True, stop=True).then_inc(ks_p, 1)
                    pe.matmul(o, qg[:, q, tok], S[:, :], start=True, stop=False)
                if phase == 1:
                    if c:
                        pe.wait_ge(w_ready, n * (NC - 1) + c)
                    else:
                        pe.wait_ge(r_ready, n * len(LEVELS) + len(LEVELS))
                    pe.matmul(US, Rf[:, q % 2, c], W[:, :] if c else Vn[:, q, 0], start=True, stop=True).then_inc(u_p, 1)
                if phase == 2:
                    pe.wait_ge(u_ready, n * NC + c + 1)
                    if c < NC - 1:
                        pe.matmul(SS, Kd[:, q, c], U[:, :], start=True, stop=True).then_inc(s_p, 1)
                    if c == 0:
                        wait_prior("O_ready", n)
                    mm = pe.matmul(o, PT[:, q, c], U[:, :], start=(c == 0), stop=True)
                    if c == NC - 1:
                        mm.then_inc(s_p, 1)

            def finish_part(slot, n, q, j):
                p = q % 2
                if slot == 2:
                    pe.wait_ge(s["on_ready"], n + 1)
                    wait_prior("lg_ready", n)
                    for c in range(NC):
                        mm = pe.transpose(PD[:, c * D:c * D + D], on[:, c], ident)
                    mm.then_inc(s["on_tp"], 1)
                if slot == 4:
                    pe.wait_ge(s["onT_ready"], n + 1)
                    for c in range(NC):
                        mm = pe.matmul(PD[:, c * D:c * D + D], onT[:, c * D:c * D + D], wo[:, :], start=True, stop=True)
                    mm.then_inc(s["oproj_p"], 1)
                if slot == 8:
                    pe.wait_ge(s["x2_ready"], n + 1)
                    for c in range(NC):
                        mm = pe.transpose(PD[:, c * D:c * D + D], x2[:, c], ident)
                    mm.then_inc(s["x2_tp"], 1)
                if slot == 10:
                    pe.wait_ge(s["x2T_ready"], n + 1)
                    pe.matmul(PD[0:EXPERTS, :], w[:, W_GATE:W_GATE + EXPERTS], x2T[:, p], start=True, stop=True
                              ).then_inc(s["logit_p"], 1)

            pe.wait_ge(wo_ready, 1)

            def iteration(gather, project, invert, scan, finish):
                for slot in range(SLOTS):
                    if invert:
                        invert_part(slot, *invert)
                    if scan:
                        scan_part(slot, *scan)
                    if project:
                        project_part(slot, *project)
                    if finish:
                        finish_part(slot, *finish)

            pipeline(pe, iteration)

            for it in range(SINKHORN):
                for h in range(2):
                    pe.wait_ge(sk[h], 5 + 4 * it + 2)
                    pe.matmul(bank[h][:, :], blockc[:, h], K2[:, h], start=True, stop=True).then_inc(rows_p[h], 1)
            DONE = 5 + 4 * SINKHORN
            for h in range(2):
                pe.wait_ge(sk[h], DONE + 2 * (TOP // 8) + 1)
                pe.matmul(bank[h][:, :], cst[:, C_HIGHER:C_HIGHER + D], r2[:, h], start=True, stop=True
                          ).then_inc(higher_p[h], 1)
            for h in range(2):
                pe.wait_ge(sk[h], DONE + 2 * (TOP // 8) + 3)
                for c in range(NC):
                    mm = pe.transpose(bank[2 + h][:, c * D:c * D + D], work2[:, h, c * D:c * D + D], ident)
                mm.then_inc(wt_p[h], 1)
            pe.wait_ge(wt_ready, 2)

            def experts(n, p, j):
                pe.wait_ge(batch_in[p], 32 * (j + 1))
                for c in range(NC):
                    if c % 2 == 0 and not (isinstance(n, int) and n == 0):
                        pe.wait_ge(acc_e[3], n * 2 - 1 + c // 2)
                        pe.wait_ge(part_ready, n * 2 - 1 + c // 2)
                    for k in range(2):
                        mm = pe.matmul(bank[2 * c + k][:, :], xb[:, p, c * D:c * D + D],
                                       w[:, W_EXP + PE_BANK * k:W_EXP + PE_BANK * (k + 1)], start=True, stop=True)
                    mm.then_inc(y_chunk, 1)

            experts(0, 0, 0)
            experts(1, 1, 0)
            with pe.Fori(1, SEQS // 2) as i:
                for p in range(2):
                    experts(i * 2 + p, p, i)

        @block.scalar
        def _(act):
            act.wait_ge(w_in, 16)
            act.activation(neg_a[:, :], w[:, W_ALOG:W_ALOG + 1], ACT.Exp).then_inc(a_exp, 1)

            def project_part(slot, n, q, j):
                if slot == 0:
                    act.wait_ge(s["x_tp"], n + 1)
                    act.activation(xT[:, :], PA[0][:, :], ACT.Copy).then_inc(s["xT_ready"], 1)
                for t, at, b, k in (("q", 1, 1, 0), ("k", 2, 0, 1), ("v", 3, 1, 2)):
                    if slot == at:
                        act.wait_ge(proj_p[t], n + 1)
                        act.activation(conv[t][:, :], PA[b][:, :], ACT.Copy,
                                       scale=w[:, W_CONV + TAPS * k + TAPS - 1:W_CONV + TAPS * k + TAPS]
                                       ).then_inc(tap[t][0], 1)
                if slot == 5:
                    for t, dst in (("q", qT[:, :]), ("k", kT[:, q]), ("v", vT[:, :])):
                        act.wait_ge(tap[t][TAPS - 1], n + 1)
                        if t == "q" and not (isinstance(n, int) and n == 0):
                            act.wait_ge(s["qg_ready"], n)
                        act.activation(dst, conv[t][:, :], ACT.Silu).then_inc(silu[t], 1)
                    act.wait_ge(s["gate_p"], n + 1)
                    act.activation(gate[:, q], chunks(PA[0][:, :]), ACT.Silu).then_inc(s["gate_ready"], 1)
                if slot == 6:
                    act.preload_act_table_set("natural_log_exp_and_others")
                    act.wait_ge(s["ab_sb"], n + 1)
                    act.activation(eb[:, :], ab[:, 1], ACT.Exp, scale=-1.0).then_inc(s["beta_e"], 1)
                    act.wait_ge(s["zabs_ready"], n + 1)
                    act.activation(ez[:, :], zabs[:, :], ACT.Exp, scale=-1.0).then_inc(s["z_exp"], 1)
                    act.wait_ge(s["z_exp"], n + 1)
                    act.activation(lz[:, :], ez[:, :], ACT.Ln, bias=1.0).then_inc(s["z_log"], 1)
                if slot == 8:
                    act.wait_ge(s["G_ready"], n + 1)
                    act.activation(gam_tok[:, q], G[:, :], ACT.Exp).then_inc(s["gam_tok_ready"], 1)
                    act.wait_ge(s["gdiff_ready"], n + 1)
                    act.activation(gexp[:, :], gdiff[:, :], ACT.Exp).then_inc(s["gexp_ready"], 1)
                    act.wait_ge(s["earg_ready"], n + 1)
                    act.wait_ge(s["Gbc_p"], n + 1)
                    if not (isinstance(n, int) and n == 0):
                        act.wait_ge(s["qg_ready"], n)
                    act.activation(gam[:, :, :], chunks(PA[1][:, :]), ACT.Exp).then_inc(s["gam_ready"], 1)
                    act.activation(E[:, :, :], earg[:, :, :], ACT.Exp).then_inc(s["E_ready"], 1)

            def invert_part(slot, n, q, j):
                L = len(LEVELS)
                if slot == 0:
                    act.wait_ge(s["t0_p"], n + 1)
                    act.activation(T[:, :, :], chunks(PT_[:, :]), ACT.Copy).then_inc(t0_ready, 1)
                elif slot % 2 == 0:
                    l = slot // 2 - 1
                    act.wait_ge(inv_p, n * L + l + 1)
                    if l < L - 1:
                        act.activation(T[:, :, :], chunks(PT_[:, :]), ACT.Copy).then_inc(t_ready, 1)
                        act.activation(Rl[:, l % 2], chunks(PR[:, :]), ACT.Copy).then_inc(r_ready, 1)
                    else:
                        act.activation(Rf[:, q % 2], chunks(PR[:, :]), ACT.Copy).then_inc(r_ready, 1)

            def scan_part(slot, n, q, j):
                c, phase = divmod(slot, 3)
                if c < NC and phase == 1:
                    act.wait_ge(u_p, n * NC + c + 1)
                    act.activation(U[:, :], US, ACT.Copy).then_inc(u_ready, 1)
                if slot == SLOTS - 1:
                    act.wait_ge(s_p, n * NC + NC)
                    act.activation(O[:, q % 2], chunks(CO[:, :]), ACT.Copy).then_inc(s["O_ready"], 1)

            def finish_part(slot, n, q, j):
                p = q % 2
                if slot == 0:
                    act.wait_ge(s["O_ready"], n + 1)
                    for c in range(NC):
                        a = act.activation(junk[:, c], O[:, p, c], ACT.Square, accum_out=so[:, c:c + 1])
                    a.then_inc(s["o_sq"], 1)
                if slot == 2:
                    act.wait_ge(s["on_tp"], n + 1)
                    act.activation(onT[:, :], PD[:, :], ACT.Copy).then_inc(s["onT_ready"], 1)
                if slot == 8:
                    act.wait_ge(s["x2_tp"], n + 1)
                    if not (isinstance(n, int) and n < 2):
                        act.wait_ge(x2_stored[p], 16 * (j * 2 + q // 2))
                    act.activation(x2T[:, p], PD[:, :], ACT.Copy).then_inc(s["x2T_ready"], 1)
                if slot == 10:
                    act.wait_ge(s["logit_p"], n + 1)
                    if not (isinstance(n, int) and n < 2):
                        act.wait_ge(lg_stored[p], 16 * (j * 2 + q // 2))
                    act.activation(lg[:, p], PD[0:EXPERTS, :], ACT.Copy).then_inc(s["lg_ready"], 1)

            def iteration(gather, project, invert, scan, finish):
                for slot in range(SLOTS):
                    if invert:
                        invert_part(slot, *invert)
                    if scan:
                        scan_part(slot, *scan)
                    if finish:
                        finish_part(slot, *finish)
                    if project:
                        project_part(slot, *project)

            pipeline(act, iteration)

            def scale(n, p):
                act.wait_ge(gcur_ready, n + 1)
                if not (isinstance(n, int) and n == 0):
                    act.wait_ge(sum_ab, n)
                for c in range(NC):
                    act.wait_ge(y_chunk, n * NC + c + 1)
                    for e in range(4):
                        a = act.activation(part[:, e, c], bank[2 * c + 1][:, e * D:e * D + D], ACT.Copy,
                                           scale=gcur[:, p, c, 4 + e:5 + e])
                    if c % 2:
                        a.then_inc(part_ready, 1)

            scale(0, 0)
            scale(1, 1)
            with act.Fori(1, SEQS // 2) as i:
                for p in range(2):
                    scale(i * 2 + p, p)

        @block.vector
        def _(dve):
            dve.wait_ge(w_in, 16)
            dve.tensor_scalar(wo[:, :], w[:, W_O:W_O + D], w[:, W_NORM:W_NORM + 1], None, ALU.mult).then_inc(wo_ready, 1)
            dve.wait_ge(a_exp, 1)
            dve.tensor_scalar(neg_a[:, :], neg_a[:, :], -1.0, None, ALU.mult).then_inc(neg_a_ready, 1)
            dve.wait_ge(neg_a_ready, 1)
            dve.wait_ge(cst_in, 16)

            def norm_stats(src, st, mv, ve, n, stats, aggr, var):
                for c in range(NC):
                    a = dve.bn_stats(st[:, c, :], src[:, c])
                a.then_inc(stats, 1)
                dve.wait_ge(stats, n + 1)
                dve.sem_inc(passed, 1)
                for c in range(NC):
                    a = dve.bn_aggr(mv[:, c, :], st[:, c, :])
                a.then_inc(aggr, 1)
                dve.wait_ge(aggr, n + 1)
                dve.tensor_scalar(ve[:, :], mv[:, :, 1], 1e-5, None, ALU.add).then_inc(var, 1)

            def normalize(src, mv, rs, dst, n, rstd_, ready):
                dve.wait_ge(rstd_, n + 1)
                for c in range(NC):
                    a = dve.tensor_scalar(dst[:, c, :], src[:, c], mv[:, c, 0:1], rs[:, c:c + 1],
                                          ALU.subtract, ALU.mult)
                a.then_inc(ready, 1)

            def taps(t, b, k, n):
                for i in range(1, TAPS):
                    dve.wait_ge(tap[t][i - 1], n + 1)
                    at = W_CONV + TAPS * k + TAPS - 1 - i
                    dve.scalar_tensor_tensor(out=conv[t][:, i:], in0=PA[b][:, 0:TOKENS - i], scalar=w[:, at:at + 1],
                                             in1=conv[t][:, i:], op0=ALU.mult, op1=ALU.add).then_inc(tap[t][i], 1)

            def project_part(slot, n, q, j):
                if slot == 0:
                    normalize(h_in[:, q], mv1, rs1, xn, n, s["ln_rstd"], s["xn_ready"])
                if slot == 1:
                    taps("q", 1, 0, n)
                if slot == 2:
                    taps("k", 0, 1, n)
                if slot == 3:
                    taps("v", 1, 2, n)
                if slot == 4:
                    dve.wait_ge(s["ab_p"], n + 1)
                    dve.tensor_copy(ab[:, :, :], AB_P.rearrange("p (c a) -> p a c", a=2)).then_inc(s["ab_sb"], 1)
                    dve.wait_ge(s["ab_sb"], n + 1)
                    dve.tensor_scalar(z[:, :], ab[:, 0], w[:, W_DT:W_DT + 1], None, ALU.add).then_inc(s["z_ready"], 1)
                    dve.wait_ge(s["z_ready"], n + 1)
                    dve.scalar_tensor_tensor(out=zabs[:, :], in0=z[:, :], scalar=-1.0, in1=z[:, :], op0=ALU.mult,
                                             op1=ALU.max).then_inc(s["zabs_ready"], 1)
                if slot == 6:
                    dve.wait_ge(s["z_log"], n + 1)
                    dve.scalar_tensor_tensor(out=sp[:, :], in0=z[:, :], scalar=0.0, in1=lz[:, :],
                                             op0=ALU.max, op1=ALU.add).then_inc(s["soft_ready"], 1)
                    dve.tensor_scalar(beta1[:, :], eb[:, :], 1.0, None, ALU.add).then_inc(s["beta_one"], 1)
                    dve.wait_ge(s["soft_ready"], n + 1)
                    dve.tensor_scalar(g[:, :], sp[:, :], neg_a[:, 0:1], None, ALU.mult).then_inc(s["g_ready"], 1)
                    dve.wait_ge(s["beta_one"], n + 1)
                    dve.reciprocal(beta[:, :], beta1[:, :]).then_inc(s["beta_ready"], 1)
                if slot == 7:
                    dve.wait_ge(s["sums_p"], n + 1)
                    dve.tensor_scalar(ss[:, :, :], SS_P, 1e-6, None, ALU.add).then_inc(s["ss_ready"], 1)
                    dve.wait_ge(s["ss_ready"], n + 1)
                    dve.reciprocal(rk[:, :], ss[:, 1]).then_inc(s["rk_ready"], 1)
                    dve.wait_ge(s["rk_ready"], n + 1)
                    dve.tensor_tensor(cj[:, :], rk[:, :], beta[:, :], ALU.mult).then_inc(s["cj_ready"], 1)
                    dve.wait_ge(s["G_p"], n + 1)
                    dve.tensor_copy(G[:, :], G_P).then_inc(s["G_ready"], 1)
                    dve.wait_ge(s["Gbc_p"], n + 1)
                    dve.wait_ge(s["G_ready"], n + 1)
                    dve.tensor_tensor(gdiff[:, :], chunks(PA[1][:, :])[:, :, D - 1], G[:, :], ALU.subtract
                                      ).then_inc(s["gdiff_ready"], 1)
                    for c in range(NC):
                        a = dve.scalar_tensor_tensor(out=earg[:, c], in0=PA[1][:, c * D:c * D + D],
                                                     scalar=G[:, c:c + 1], in1=below, op0=ALU.subtract, op1=ALU.min)
                    a.then_inc(s["earg_ready"], 1)
                if slot == 9:
                    dve.wait_ge(s["rss_ready"], n + 1)
                    dve.tensor_scalar(rq[:, q], rss[:, 0], float(D) ** -0.5, None, ALU.mult)
                    dve.tensor_tensor(knorm[:, :], ss[:, 1], rss[:, 1], ALU.mult).then_inc(s["knorm_ready"], 1)
                    dve.wait_ge(s["gexp_ready"], n + 1)
                    dve.tensor_tensor(kdec[:, :], gexp[:, :], cj[:, :], ALU.mult).then_inc(s["kdec_ready"], 1)
                    dve.wait_ge(s["gam_ready"], n + 1)
                    dve.tensor_copy(gam_end[:, q], gam[:, :, D - 1])
                    dve.wait_ge(s["kk_p"], n + 1)
                    dve.wait_ge(s["E_ready"], n + 1)
                    for c in range(NC):
                        a = dve.scalar_tensor_tensor(out=Braw[:, c], in0=PA[0][:, c * D:c * D + D],
                                                     scalar=cj[:, c:c + 1], in1=E[:, c], op0=ALU.mult, op1=ALU.mult)
                    a.then_inc(s["braw_ready"], 1)
                if slot == 10:
                    dve.wait_ge(s["kq_p"], n + 1)
                    for c in range(NC):
                        a = dve.scalar_tensor_tensor(out=PT[:, q, c], in0=PA[1][:, c * D:c * D + D],
                                                     scalar=cj[:, c:c + 1], in1=E[:, c], op0=ALU.mult, op1=ALU.mult)
                    a.then_inc(s["PT_ready"], 1)
                if slot == 11:
                    dve.wait_ge(s["ktm_p"], n + 1)
                    dve.wait_ge(s["kdec_ready"], n + 1)
                    dve.tensor_tensor(Kd[:, q], chunks(PA[0][:, :]), kdec[:, :].unsqueeze(2).broadcast_to([D, NC, D]),
                                      ALU.mult).then_inc(s["kd_ready"], 1)
                if slot == 12:
                    dve.wait_ge(s["vtm_p"], n + 1)
                    dve.wait_ge(s["knorm_ready"], n + 1)
                    dve.tensor_tensor(Vn[:, q], chunks(PA[1][:, :]), knorm[:, :].unsqueeze(2).broadcast_to([D, NC, D]),
                                      ALU.mult).then_inc(s["vn_ready"], 1)

            def invert_part(slot, n, q, j):
                L = len(LEVELS)
                if slot % 2 == 1:
                    l = slot // 2
                    dve.wait_ge(y_p, n * L + l + 1)
                    at = C_LEVEL + l * D
                    dve.tensor_tensor(Ym[:, :, :], chunks(PY[:, :]), cst[:, at:at + D].unsqueeze(1).broadcast_to([D, NC, D]),
                                      ALU.mult).then_inc(ym_ready, 1)

            def scan_part(slot, n, q, j):
                if slot >= 3 * NC:
                    return
                c, phase = divmod(slot, 3)
                if phase == 0 and c:
                    dve.wait_ge(ks_p, n * (NC - 1) + c)
                    dve.scalar_tensor_tensor(out=W[:, :], in0=KS, scalar=gam_tok[:, q, c:c + 1], in1=Vn[:, q, c],
                                             op0=ALU.mult, op1=ALU.subtract, reverse1=True).then_inc(w_ready, 1)
                if phase == 2 and c < NC - 1:
                    dve.wait_ge(s_p, n * NC + c + 1)
                    if c == 0:
                        dve.tensor_copy(S[:, :], SS).then_inc(s_ready, 1)
                    else:
                        dve.wait_ge(s_ready, n * (NC - 1) + c)
                        dve.scalar_tensor_tensor(out=S[:, :], in0=S[:, :], scalar=gam_end[:, q, c:c + 1], in1=SS,
                                                 op0=ALU.mult, op1=ALU.add).then_inc(s_ready, 1)

            def finish_part(slot, n, q, j):
                p = q % 2
                if slot == 0:
                    dve.tensor_tensor(rq2[:, :], rq[:, q], rq[:, q], ALU.mult).then_inc(s["rq2_ready"], 1)
                    dve.wait_ge(s["o_sq"], n + 1)
                    dve.wait_ge(s["rq2_ready"], n + 1)
                    dve.tensor_tensor(ms[:, :], so[:, :], rq2[:, :], ALU.mult).then_inc(s["ms_ready"], 1)
                    dve.wait_ge(s["ms_ready"], n + 1)
                    dve.tensor_scalar(ms1[:, :], ms[:, :], 1.0 / D, 1e-5, ALU.mult, ALU.add).then_inc(s["ms1_ready"], 1)
                if slot == 1:
                    dve.wait_ge(s["rstd_ready"], n + 1)
                    dve.tensor_tensor(fo[:, :], rstd[:, :], rq[:, q], ALU.mult).then_inc(s["fo_ready"], 1)
                    dve.wait_ge(s["fo_ready"], n + 1)
                    for c in range(NC):
                        a = dve.scalar_tensor_tensor(out=on[:, c], in0=O[:, p, c], scalar=fo[:, c:c + 1],
                                                     in1=gate[:, q, c], op0=ALU.mult, op1=ALU.mult)
                    a.then_inc(s["on_ready"], 1)
                if slot == 5:
                    dve.wait_ge(s["oproj_p"], n + 1)
                    if not (isinstance(n, int) and n < 2):
                        dve.wait_ge(h2_stored[p], 16 * (j * 2 + q // 2))
                    dve.tensor_tensor(h2[:, p], chunks(PD[:, :]), h_in[:, q], ALU.add).then_inc(s["h2_ready"], 1)
                    dve.wait_ge(s["h2_ready"], n + 1)
                    norm_stats(h2[:, p], st2, mv2, ve2, n, s["ln2_stats"], s["ln2_aggr"], s["ln2_var"])
                if slot == 6:
                    normalize(h2[:, p], mv2, rs2, x2, n, s["ln2_rstd"], s["x2_ready"])

            def iteration(gather, project, invert, scan, finish):
                if project:
                    n, q, j = project
                    dve.wait_ge(gathered[q], 16 * NC * (j + 1))
                    norm_stats(h_in[:, q], st1, mv1, ve1, n, s["ln_stats"], s["ln_aggr"], s["ln_var"])
                for slot in range(SLOTS):
                    if invert:
                        invert_part(slot, *invert)
                    if scan:
                        scan_part(slot, *scan)
                    if finish:
                        finish_part(slot, *finish)
                    if project:
                        project_part(slot, *project)

            pipeline(dve, iteration)

            count = [0, 0]

            def link(h, ins):
                count[h] += 1
                ins.then_inc(sk[h], 1)

            def after(h):
                dve.wait_ge(sk[h], count[h])

            for h in range(2):
                dve.wait_ge(k_in[h], 16)
                link(h, dve.tensor_scalar(K2[:, h], K2[:, h], 1e-6, None, ALU.max))
            for h in range(2):
                after(h)
                link(h, dve.tensor_reduce(col2[:, h, 0:1], K2[:, h], AX.X, ALU.max))
            for h in range(2):
                after(h)
                link(h, dve.reciprocal(col2[:, h, 1:2], col2[:, h, 0:1]))
            for h in range(2):
                after(h)
                link(h, dve.tensor_scalar(K2[:, h], K2[:, h], col2[:, h, 1:2], None, ALU.mult))
            for h in range(2):
                after(h)
                link(h, dve.tensor_reduce(col2[:, h, 2:3], K2[:, h], AX.X, ALU.add))
            for it in range(SINKHORN):
                for h in range(2):
                    after(h)
                    link(h, dve.reciprocal(col2[:, h, 3:4], col2[:, h, 2:3]))
                for h in range(2):
                    after(h)
                    link(h, dve.tensor_scalar(blockc[:, h], cst[:, C_BLOCK:C_BLOCK + D], col2[:, h, 3:4], None,
                                              ALU.mult))
                for h in range(2):
                    dve.wait_ge(rows_p[h], it + 1)
                    link(h, dve.reciprocal(r2[:, h], bank[h][:, :]))
                for h in range(2):
                    after(h)
                    if it < SINKHORN - 1:
                        link(h, dve.tensor_tensor_reduce(prod2[:, h], K2[:, h], r2[:, h], 1.0, 0.0, ALU.mult,
                                                         ALU.add, col2[:, h, 2:3]))
                    else:
                        link(h, dve.scalar_tensor_tensor(out=gates2[:, h], in0=K2[:, h], scalar=col2[:, h, 3:4],
                                                         in1=r2[:, h], op0=ALU.mult, op1=ALU.mult))
            for k in range(TOP // 8):
                src = work2 if k else gates2
                for h in range(2):
                    after(h)
                    link(h, dve.max(top8[:, h], src[:, h]))
                for h in range(2):
                    after(h)
                    link(h, dve.match_replace(work2[:, h], top8[:, h], src[:, h], -1.0))
            for h in range(2):
                after(h)
                link(h, dve.tensor_scalar(r2[:, h], work2[:, h], 0.0, None, ALU.is_lt))
            for h in range(2):
                after(h)
                link(h, dve.tensor_tensor(prod2[:, h], gates2[:, h], r2[:, h], ALU.mult))
            for h in range(2):
                after(h)
                dve.wait_ge(higher_p[h], 1)
                link(h, dve.scalar_tensor_tensor(out=work2[:, h], in0=bank[h][:, :], scalar=0.5, in1=prod2[:, h],
                                                 op0=ALU.is_lt, op1=ALU.mult))
            for h in range(2):
                dve.wait_ge(wt_p[h], 1)
                for c in range(NC):
                    a = dve.tensor_copy(wt[:, HALF * h:HALF * h + HALF, c, :],
                                        bank[2 + h][:, c * D:c * D + D].rearrange("p (b e) -> p b e", e=EXPERTS))
                a.then_inc(wt_ready, 1)
            dve.wait_ge(wt_ready, 2)

            def combine(n, p, j):
                first = isinstance(n, int) and n < 2
                dve.tensor_copy(gcur[:, p], wt[:, bass.ds(n, 1)].rearrange("p a c e -> p (a c) e")
                                ).then_inc(gcur_ready, 1)
                dve.wait_ge(batch_in[p], 32 * (j + 1))
                dve.wait_ge(gcur_ready, n + 1)
                for pair in range(NC // 2):
                    dve.wait_ge(y_chunk, n * NC + 2 * pair + 2)
                    for e in range(4):
                        if e:
                            dve.wait_ge(acc_e[e - 1], n * 2 + pair + 1)
                        for c in (2 * pair, 2 * pair + 1):
                            a = dve.scalar_tensor_tensor(out=acc[:, p, c], in0=bank[2 * c][:, e * D:e * D + D],
                                                         scalar=gcur[:, p, c, e:e + 1],
                                                         in1=acc[:, p, c] if e else hb[:, p, c],
                                                         op0=ALU.mult, op1=ALU.add)
                        a.then_inc(acc_e[e], 1)
                if not first:
                    dve.wait_ge(out_stored[p], 16 * j)
                dve.wait_ge(sum_c, n + 1)
                dve.wait_ge(acc_e[3], n * 2 + 2)
                dve.tensor_tensor(ob[:, p], acc[:, p], sums[:, 2], ALU.add).then_inc(out_ready, 1)

            combine(0, 0, 0)
            combine(1, 1, 0)
            with dve.Fori(1, SEQS // 2) as i:
                for p in range(2):
                    combine(i * 2 + p, p, i)


def kernel(**inputs):
    import numpy as _np
    import concourse.bacc as _bacc
    from concourse import mybir as _mybir
    from concourse.bass_utils import run_bass_kernel_spmd as _run

    x = _np.asarray(inputs["x"])
    a = {k: _np.asarray(v) for k, v in inputs.items()}
    ids = _np.ascontiguousarray(x.reshape(SEQS * NC, CHUNK).T)
    packed = _np.concatenate(
        [a[f"L0_attn_{k}_proj_w"].T for k in "qkvgo"]
        + [a["L0_attn_a_proj_w"].T, a["L0_attn_b_proj_w"].T]
        + [a[f"L0_attn_{k}_conv_w"] for k in "qkv"]
        + [a["L0_attn_o_norm_w"].reshape(D, 1)]
        + [_np.broadcast_to(a["L0_attn_A_log"].reshape(1, 1), (D, 1)),
           _np.broadcast_to(a["L0_attn_dt_bias"].reshape(1, 1), (D, 1))]
        + [a["L0_ffn_gate_weight"].reshape(D, EXPERTS)]
        + [a["L0_ffn_experts"].transpose(1, 0, 2).reshape(D, EXPERTS * D)], axis=1)
    arrays = {
        "ids_dram": ids,
        "table_dram": _np.ascontiguousarray(a["L0_tok_idx2vec"]),
        "weights_dram": _np.ascontiguousarray(packed),
        "consts_dram": shape_constants(),
    }
    nc = _bacc.Bacc("TRN2", target_bir_lowering=False, num_devices=1)
    args = [nc.dram_tensor(k, v.shape, _mybir.dt.from_np(v.dtype), kind="ExternalInput").ap() for k, v in arrays.items()]
    f32 = _mybir.dt.float32
    out = nc.dram_tensor("out_dram", (SEQS, TOKENS, D), f32, kind="ExternalOutput").ap()
    x2 = nc.dram_tensor("x2_dram", (SEQS, D, TOKENS), f32, kind="Internal").ap()
    h2 = nc.dram_tensor("h2_dram", (SEQS, D, TOKENS), f32, kind="Internal").ap()
    logit = nc.dram_tensor("logit_dram", (SEQS * EXPERTS, TOKENS), f32, kind="Internal").ap()
    tower(nc, *args, out, x2, h2, logit)
    r = _run(nc, [arrays], core_ids=[0])
    return r.results[0]["out_dram"]
```

```python
from contextlib import ExitStack

import concourse.bass as bass
import numpy as np
from concourse import mybir

SEQS, TOKENS, D = 32, 512, 128
VOCAB = 50257
CHUNK = 128
NC = TOKENS // CHUNK
EXPERTS = 8
TOP = TOKENS // EXPERTS
TAPS = 4
SINKHORN = 8
HALF = 128 // EXPERTS
LEVELS = (2, 4, 8, 16, 32, 64)
RING = 4
H = CHUNK // 2
SLOTS = 13
STAGES = 6
PE_BANK = 512

W_Q, W_K, W_V, W_O, W_G = (D * i for i in range(5))
W_AB = 5 * D
W_CONV = W_AB + 2
W_NORM = W_CONV + 3 * TAPS
W_ALOG = W_NORM + 1
W_DT = W_ALOG + 1
W_GATE = W_DT + 1
W_EXP = W_GATE + EXPERTS
W_COLS = W_EXP + EXPERTS * D
C_ID, C_TRI, C_NEG, C_BLOCK, C_HIGHER, C_PAIR, C_LEVEL = (D * i for i in range(7))
C_COLS = C_LEVEL + len(LEVELS) * D


def shape_constants():
    r = np.arange(D)
    row, col = r[:, None], r[None, :]

    def doubling(w):
        same = row // (2 * w) == col // (2 * w)
        return np.eye(D) - (same & (row // w % 2 == 1) & (col // w % 2 == 0))

    blocks = [
        np.eye(D),
        row <= col,
        np.where(row <= col, 0.0, -1e30),
        row // EXPERTS == col // EXPERTS,
        (row // EXPERTS == col // EXPERTS) & (row > col),
        doubling(1).T,
    ] + [doubling(w) for w in LEVELS]
    return np.concatenate([b.astype(np.float32) for b in blocks], axis=1)


def tower(nc, ids_d, table_d, weights_d, consts_d, out_d, x2_d, logit_d):
    F32 = mybir.dt.float32
    I32 = mybir.dt.int32
    ALU = mybir.AluOpType
    ACT = mybir.ActivationFunctionType
    AX = mybir.AxisListType

    ctx = ExitStack()
    with ctx:
        def sb(name, shape, dt=F32):
            return ctx.enter_context(nc.sbuf_tensor(name, shape, dt))

        def sem(name):
            return ctx.enter_context(nc.semaphore(name))

        w = sb("w", [D, W_COLS])
        cst = sb("cst", [D, C_COLS])
        ids = sb("ids", [D, SEQS * NC], I32)
        wo = sb("wo", [D, D])
        neg_a = sb("neg_a", [D, 1])
        ident = cst[:, C_ID:C_ID + D]
        tri = cst[:, C_TRI:C_TRI + D]
        ones = cst[:, C_TRI + D - 1:C_TRI + D]
        below = cst[:, C_NEG:C_NEG + D]
        idx = sb("idx", [D, 2, NC], I32)
        h_in = sb("h_in", [D, 2, NC, D])
        hall = sb("hall", [D, SEQS, NC, D])
        st1 = sb("st1", [D, NC, 6])
        mv1 = sb("mv1", [D, NC, 2])
        ve1 = sb("ve1", [D, NC])
        rs1 = sb("rs1", [D, NC])
        xn = sb("xn", [D, NC, D])
        xT = sb("xT", [D, TOKENS])
        conv = {s: sb("conv_" + s, [D, TOKENS]) for s in "qkv"}
        qT = sb("qT", [D, 2, TOKENS])
        kT = sb("kT", [D, RING, TOKENS])
        vT = sb("vT", [D, 2, TOKENS])
        gate = sb("gate", [D, RING, NC, D])
        sq = sb("sq", [D, TOKENS])
        ab = sb("ab", [D, 2, NC])
        z = sb("z", [D, NC])
        zabs = sb("zabs", [D, NC])
        eb = sb("eb", [D, NC])
        ez = sb("ez", [D, NC])
        lz = sb("lz", [D, NC])
        beta = sb("beta", [D, NC])
        beta1 = sb("beta1", [D, NC])
        sp = sb("sp", [D, NC])
        g = sb("g", [D, NC])
        G = sb("G", [D, NC])
        ssk = sb("ssk", [D, NC])
        ss = sb("ss", [D, NC])
        rss = sb("rss", [D, NC])
        minus_half = sb("minus_half", [D, NC])
        rk = sb("rk", [D, NC])
        cj = sb("cj", [D, NC])
        knorm = sb("knorm", [D, NC])
        eps_q = sb("eps_q", [D, RING, NC])
        gdiff = sb("gdiff", [D, NC])
        gexp = sb("gexp", [D, NC])
        kdec = sb("kdec", [D, NC])
        earg = sb("earg", [D, NC, D])
        E = sb("E", [D, NC, D])
        Ec = sb("Ec", [D, NC, D])
        gam = sb("gam", [D, NC, D])
        gam_tok = sb("gam_tok", [D, RING, NC])
        gam_end = sb("gam_end", [D, RING, NC])
        qg = sb("qg", [D, RING, TOKENS])
        PT = sb("PT", [D, RING, NC, D])
        Kd = sb("Kd", [D, RING, NC, D])
        Vn = sb("Vn", [D, RING, NC, D])
        Braw = sb("Braw", [D, NC, D])
        Bt = sb("Bt", [D, 2, NC, D])
        R0 = sb("R0", [D, 2, NC, D])
        Rl = sb("Rl", [D, 2, NC, D])
        Rf = sb("Rf", [D, 2, NC, D])
        T = sb("T", [D, NC, D])
        Ym = sb("Ym", [D, NC, D])
        S = sb("S", [D, D])
        W = sb("W", [D, D])
        U = sb("U", [D, D])
        O = sb("O", [D, 2, NC, D])
        junk = sb("junk", [D, NC, D])
        so = sb("so", [D, NC])
        ms1 = sb("ms1", [D, NC])
        rstd = sb("rstd", [D, NC])
        on = sb("on", [D, NC, D])
        onT = sb("onT", [D, TOKENS])
        st2 = sb("st2", [D, NC, 6])
        mv2 = sb("mv2", [D, NC, 2])
        ve2 = sb("ve2", [D, NC])
        rs2 = sb("rs2", [D, NC])
        x2 = sb("x2", [D, NC, D])
        x2T = sb("x2T", [D, 2, TOKENS])
        lg = sb("lg", [EXPERTS, 2, TOKENS])
        K2 = Rl[:, :, :, :].rearrange("p a c d -> p a (c d)")
        r2 = Bt[:, :, :, :].rearrange("p a c d -> p a (c d)")
        gates2 = R0[:, :, :, :].rearrange("p a c d -> p a (c d)")
        work2 = Rf[:, :, :, :].rearrange("p a c d -> p a (c d)")
        prod2 = O[:, :, :, :].rearrange("p a c d -> p a (c d)")
        blockc = gam[:, 0:2, :]
        col2 = sb("col2", [D, 2, 4])
        K2T = PT[:, 2:4, :, :]
        owner = cst[:, C_BLOCK:C_BLOCK + D].rearrange("p (b e) -> p b e", e=EXPERTS)[:, :, 0]
        c16 = sb("c16", [D, 2, HALF])
        r_tok = sb("r_tok", [D, 2, NC * HALF])
        own = sb("own", [D, 2, HALF])
        top8 = sb("top8", [D, 2, 8])
        wt = sb("wt", [D, SEQS, NC, EXPERTS])
        gcur = sb("gcur", [D, 2, NC, EXPERTS])
        xb = kT[:, :, :]
        acc = PT[:, 0:2, :, :]
        part = (Kd, gate)
        sums = Vn[:, 0:3, :, :]
        ob = qg[:, 0:2, :].rearrange("p a (c d) -> p a c d", d=D)

        bank = [ctx.enter_context(nc.psum_tensor(f"bank{i}", [D, PE_BANK], F32)) for i in range(8)]
        PA = bank[0:2]
        PR, PT_, PM = bank[2:5]
        PY = PT_
        CW, CO, PD = bank[5:8]
        KS, US, SS = CW[:, 0:D], CW[:, D:2 * D], CW[:, 2 * D:3 * D]
        SS_P = PM[:, 2 * D:2 * D + NC]
        G_P = PM[:, 3 * D:3 * D + NC]
        GATE = D + 2

        def chunks(ap):
            return ap.rearrange("p (c d) -> p c d", d=D)

        ids_in, w_in, cst_in = sem("ids_in"), sem("w_in"), sem("cst_in")
        half_ready = sem("half_ready")
        passed = sem("passed")
        wo_ready, a_exp, neg_a_ready = sem("wo_ready"), sem("a_exp"), sem("neg_a_ready")
        idx_ready = sem("idx_ready")
        gathered = [sem(f"gathered{i}") for i in range(2)]
        hall_in = [sem(f"hall_in{i}") for i in range(2)]
        names = """ln_stats ln_aggr ln_var ln_rstd x_centered xn_ready x_tp xT_ready gate_p ab_sb
            gate_ready sums_p beta_e z_ready zabs_ready z_exp z_log beta_one beta_ready soft_ready
            g_ready G_p Gbc_p G_ready epsq_ready ssk_ready ss_ready rss_ready rk_ready cj_ready knorm_ready
            gdiff_ready gexp_ready kdec_ready earg_ready E_ready Ec_ready gam_ready gam_tok_ready
            qg_ready kk_p kq_p braw_ready bt_ready PT_ready r0_ready ktm_p vtm_p kd_ready vn_ready
            t0_p O_ready o_sq ms1_ready rstd_ready on_ready on_tp onT_ready
            oproj_p h2_ready ln2_stats ln2_aggr ln2_var ln2_rstd x2_ready x2_tp x2T_ready logit_p lg_ready""".split()
        s = {n: sem(n) for n in names}
        proj_p = {t: sem(f"proj_{t}") for t in "qkv"}
        tap = {t: [sem(f"tap_{t}{i}") for i in range(TAPS)] for t in "qkv"}
        silu = {t: sem(f"silu_{t}") for t in "qkv"}
        squared = sem("squared")
        y_p, ym_ready, t_p, r_p, r_ready, t_ready = (
            sem(x) for x in ("y_p", "ym_ready", "t_p", "r_p", "r_ready", "t_ready"))
        t0_ready = sem("t0_ready")
        ks_p, w_ready, u_p, u_ready, s_p, s_ready = (
            sem(x) for x in ("ks_p", "w_ready", "u_p", "u_ready", "s_p", "s_ready"))
        x2_stored = [sem(f"x2_stored{i}") for i in range(2)]
        lg_stored = [sem(f"lg_stored{i}") for i in range(2)]
        k_in = [sem(f"k_in{h}") for h in range(2)]
        sk = [sem(f"sinkhorn{h}") for h in range(2)]
        rows_p = [sem(f"rows_p{h}") for h in range(2)]
        kt_p = [sem(f"kt_p{h}") for h in range(2)]
        kt_ready = [sem(f"kt_ready{h}") for h in range(2)]
        cols_p = [sem(f"cols_p{h}") for h in range(2)]
        higher_p = [sem(f"higher_p{h}") for h in range(2)]
        wt_p = [sem(f"wt_p{h}") for h in range(2)]
        wt_ready = sem("wt_ready")
        batch_in = [sem(f"batch_in{i}") for i in range(RING)]
        gcur_ready = sem("gcur_ready")
        y_chunk = sem("y_chunk")
        part_ready = sem("part_ready")
        acc_e = [sem(f"acc_e{e}") for e in range(4)]
        sum_ab, sum_c = sem("sum_ab"), sem("sum_c")
        out_ready = sem("out_ready")
        out_stored = [sem(f"out_stored{i}") for i in range(2)]

        def loop(engine, start, end):
            return nc.Fori(start, end, engines=bass.OrderedEngineSet([engine.engine]), hint_back_edge=True)

        def stages(i, u):
            found = []
            for k in range(STAGES):
                q = (u - k) % RING
                j = i + (u - k - q) // RING
                n = j * RING + q
                found.append((n, q, j) if not isinstance(n, int) or 0 <= n < SEQS else None)
            return found

        def pipeline(engine, iteration):
            for u in range(2 * RING):
                iteration(*stages(u // RING, u % RING))
            with loop(engine, 2, SEQS // RING) as i:
                for u in range(RING):
                    iteration(*stages(i, u))
            for t in range(SEQS, SEQS + STAGES - 1):
                iteration(*stages(t // RING, t % RING))

        def sequences(engine, step):
            for q in range(RING):
                step(q, q, 0)
            with loop(engine, 1, SEQS // RING) as i:
                for q in range(RING):
                    step(i * RING + q, q, i)

        def uses(q, j):
            return j * (RING // 2) + q // 2 + 1

        block = ctx.enter_context(nc.Block())

        @block.sync
        def _(sp_):
            sp_.dma_start(ids[:, :], ids_d).then_inc(ids_in, 16)
            sp_.dma_start(w[:, :], weights_d).then_inc(w_in, 16)
            sp_.dma_start(cst[:, :], consts_d).then_inc(cst_in, 16)

            def iteration(gather, project, product, invert, scan, finish):
                if gather:
                    n, q, j = gather
                    p = q % 2
                    sp_.wait_ge(gathered[p], 16 * NC * uses(q, j))
                    sp_.dma_start(hall[:, bass.ds(n, 1)].rearrange("p a c d -> p (a c d)"),
                                  h_in[:, p].rearrange("p c d -> p (c d)")).then_inc(hall_in[p], 16)
                if finish:
                    n, q, j = finish
                    p = q % 2
                    sp_.wait_ge(s["x2T_ready"], n + 1)
                    sp_.dma_start(x2_d[bass.ds(n, 1)].rearrange("a p x -> (a p) x"), x2T[:, p]).then_inc(x2_stored[p], 16)
                    sp_.wait_ge(s["lg_ready"], n + 1)
                    sp_.dma_start(logit_d[bass.ds(n * EXPERTS, EXPERTS)], lg[:, p]).then_inc(lg_stored[p], 16)

            pipeline(sp_, iteration)
            for i in range(2):
                sp_.wait_ge(x2_stored[i], 16 * (SEQS // 2))
                sp_.wait_ge(lg_stored[i], 16 * (SEQS // 2))
            for h in range(2):
                sp_.dma_start(K2[:, h], logit_d[D * h:D * h + D]).then_inc(k_in[h], 16)

            def load(n, q):
                sp_.dma_start(xb[:, q], x2_d[bass.ds(n, 1)].rearrange("a p x -> (a p) x")).then_inc(batch_in[q], 16)

            def store(n, p):
                sp_.wait_ge(out_ready, n + 1)
                sp_.dma_start(out_d[bass.ds(n, 1)].rearrange("a (c p) d -> p (a c) d", p=CHUNK),
                              ob[:, p]).then_inc(out_stored[p], 16)

            for q in range(RING):
                load(q, q)
            with loop(sp_, 0, SEQS // RING - 1) as i:
                for q in range(RING):
                    n = i * RING + q
                    sp_.wait_ge(y_chunk, n * NC + NC)
                    load(n + RING, q)
                    store(n, q % 2)
            for q in range(RING):
                store(SEQS - RING + q, q % 2)
            for p in range(2):
                sp_.wait_ge(out_stored[p], 16 * (SEQS // 2))

        @block.gpsimd
        def _(pool):
            pool.memset(minus_half[:, :], -0.5).then_inc(half_ready, 1)
            pool.wait_ge(half_ready, 1)
            pool.wait_ge(ids_in, 16)

            def inverse_root(dst, src, n, src_ready, dst_ready):
                pool.wait_ge(src_ready, n + 1)
                pool.tensor_tensor(dst, src, minus_half[:, :], ALU.pow).then_inc(dst_ready, 1)

            def rows(n, q, j):
                p = q % 2
                if not (isinstance(n, int) and n < 2):
                    pool.wait_ge(s["xn_ready"], n - 1)
                    pool.wait_ge(hall_in[p], 16 * (uses(q, j) - 1))
                    pool.sem_inc(passed, 1)
                pool.tensor_copy(idx[:, p], ids[:, bass.ds(n * NC, NC)]).then_inc(idx_ready, 1)
                pool.wait_ge(idx_ready, n + 1)
                pool.sem_inc(passed, 1)
                for c in range(NC):
                    pool.indirect_dma_start(out=h_in[:, p, c, :], out_offset=None, in_=table_d,
                                            in_offset=bass.IndirectOffsetOnAxis(ap=idx[:, p, c:c + 1], axis=0)
                                            ).then_inc(gathered[p], 16)

            def iteration(gather, project, product, invert, scan, finish):
                if finish:
                    inverse_root(rstd[:, :], ms1[:, :], finish[0], s["ms1_ready"], s["rstd_ready"])
                if gather:
                    rows(*gather)
                if product:
                    n, q, j = product
                    pool.wait_ge(s["gam_ready"], n + 1)
                    pool.tensor_tensor(qg[:, q], qT[:, q % 2], gam[:, :, :].rearrange("p c d -> p (c d)"),
                                       ALU.mult).then_inc(s["qg_ready"], 1)
                    inverse_root(rss[:, :], ss[:, :], n, s["ss_ready"], s["rss_ready"])
                    pool.wait_ge(s["braw_ready"], n + 1)
                    pool.sem_inc(passed, 1)
                    pool.affine_select(out=Bt[:, q % 2], in_=Braw[:, :, :], compare_op=ALU.not_equal, fill=1.0,
                                       base=0, pattern=[[0, NC], [-1, D]],
                                       channel_multiplier=1).then_inc(s["bt_ready"], 1)
                    pool.wait_ge(s["cj_ready"], n + 1)
                    pool.wait_ge(s["E_ready"], n + 1)
                    pool.tensor_tensor(Ec[:, :, :], E[:, :, :], cj[:, :].unsqueeze(2).broadcast_to([D, NC, D]),
                                       ALU.mult).then_inc(s["Ec_ready"], 1)
                if finish:
                    inverse_root(rs2[:, :], ve2[:, :], finish[0], s["ln2_var"], s["ln2_rstd"])
                if gather:
                    n, q, j = gather
                    inverse_root(rs1[:, :], ve1[:, :], n, s["ln_var"], s["ln_rstd"])
                    if not (isinstance(n, int) and n == 0):
                        pool.wait_ge(s["x_tp"], n)
                    pool.tensor_tensor(xn[:, :, :], h_in[:, q % 2], mv1[:, :, 0:1].broadcast_to([D, NC, D]),
                                       ALU.subtract).then_inc(s["x_centered"], 1)
                    pool.wait_ge(s["x_centered"], n + 1)
                    pool.wait_ge(s["ln_rstd"], n + 1)
                    pool.tensor_tensor(xn[:, :, :], xn[:, :, :], rs1[:, :].unsqueeze(2).broadcast_to([D, NC, D]),
                                       ALU.mult).then_inc(s["xn_ready"], 1)
                if product:
                    n, q, j = product
                    pool.wait_ge(s["bt_ready"], n + 1)
                    if isinstance(n, int) and n == 0:
                        pool.wait_ge(cst_in, 16)
                    pool.tensor_tensor(R0[:, q % 2], Bt[:, q % 2],
                                       cst[:, C_PAIR:C_PAIR + D].unsqueeze(1).broadcast_to([D, NC, D]),
                                       ALU.mult).then_inc(s["r0_ready"], 1)
                if project:
                    n, q, j = project
                    pool.wait_ge(silu["q"], n + 1)
                    if not (isinstance(n, int) and n == 0):
                        pool.wait_ge(s["sums_p"], n)
                    pool.tensor_tensor(sq[:, :], qT[:, q % 2], qT[:, q % 2], ALU.mult).then_inc(squared, 1)

            pipeline(pool, iteration)

            def add(n, q, j):
                p = q % 2
                pool.wait_ge(part_ready, n * 2 + 2)
                pool.tensor_tensor(sums[:, 0], part[p][:, 0], part[p][:, 1], ALU.add)
                pool.tensor_tensor(sums[:, 1], part[p][:, 2], part[p][:, 3], ALU.add).then_inc(sum_ab, 1)
                pool.wait_ge(sum_ab, n + 1)
                pool.tensor_tensor(sums[:, 2], sums[:, 0], sums[:, 1], ALU.add).then_inc(sum_c, 1)
                pool.wait_ge(sum_c, n + 1)
                pool.wait_ge(acc_e[3], n * 2 + 2)
                if not (isinstance(n, int) and n < 2):
                    pool.wait_ge(out_stored[p], 16 * (uses(q, j) - 1))
                    pool.sem_inc(passed, 1)
                pool.tensor_tensor(ob[:, p], acc[:, p], sums[:, 2], ALU.add).then_inc(out_ready, 1)

            sequences(pool, add)

        @block.tensor
        def _(pe):
            pe.wait_ge(w_in, 16)
            pe.wait_ge(cst_in, 16)

            def wait_prior(name, n):
                if not (isinstance(n, int) and n == 0):
                    pe.wait_ge(s[name], n)

            def cols(c):
                return slice(c * D, c * D + D)

            def gather_part(slot, n, q, j):
                if slot == 11:
                    pe.wait_ge(s["xn_ready"], n + 1)
                    wait_prior("gate_ready", n)
                    for c in range(NC):
                        mm = pe.transpose(PA[0][:, cols(c)], xn[:, c, :], ident)
                    mm.then_inc(s["x_tp"], 1)

            def project_part(slot, n, q, j):
                if slot == 0:
                    pe.wait_ge(s["xT_ready"], n + 1)
                    pe.matmul(PA[0][:, :], w[:, W_Q:W_Q + D], xT[:, :], start=True, stop=True).then_inc(proj_p["q"], 1)
                if slot == 3:
                    pe.wait_ge(tap["q"][TAPS - 1], n + 1)
                    pe.matmul(PA[0][:, :], w[:, W_K:W_K + D], xT[:, :], start=True, stop=True).then_inc(proj_p["k"], 1)
                if slot == 6:
                    pe.wait_ge(tap["k"][TAPS - 1], n + 1)
                    pe.matmul(PA[0][:, :], w[:, W_V:W_V + D], xT[:, :], start=True, stop=True).then_inc(proj_p["v"], 1)
                if slot == 9:
                    pe.wait_ge(tap["v"][TAPS - 1], n + 1)
                    wait_prior("epsq_ready", n)
                    for c in range(NC):
                        at = PA[0][:, c * GATE:c * GATE + GATE] if c < NC - 1 else PM[:, 0:GATE]
                        mm = pe.matmul(at, xT[:, cols(c)], w[:, W_G:W_G + GATE], start=True, stop=True)
                    mm.then_inc(s["gate_p"], 1)

            def product_part(slot, n, q, j):
                if slot == 0:
                    pe.wait_ge(s["g_ready"], n + 1)
                    pe.wait_ge(s["gate_ready"], n + 1)
                    pe.matmul(G_P, tri, g[:, :], start=True, stop=True).then_inc(s["G_p"], 1)
                if slot == 1:
                    wait_prior("vn_ready", n)
                    for c in range(NC):
                        mm = pe.matmul(PA[1][:, cols(c)], g[:, c:c + 1].broadcast_to([D, D]), tri, start=True, stop=True)
                    mm.then_inc(s["Gbc_p"], 1)
                if slot == 2:
                    pe.wait_ge(s["G_ready"], n + 1)
                    pe.wait_ge(squared, n + 1)
                    for c in range(NC):
                        mm = pe.matmul(SS_P[:, c:c + 1], sq[:, cols(c)], ones, start=True, stop=True)
                    mm.then_inc(s["sums_p"], 1)
                if slot == 3:
                    pe.wait_ge(s["gam_ready"], n + 1)
                    for c in range(NC):
                        mm = pe.matmul(PA[1][:, cols(c)], kT[:, q, cols(c)], kT[:, q, cols(c)], start=True, stop=True)
                    mm.then_inc(s["kk_p"], 1)
                if slot == 8:
                    pe.wait_ge(s["braw_ready"], n + 1)
                    for c in range(NC):
                        mm = pe.matmul(PA[1][:, cols(c)], kT[:, q, cols(c)], qT[:, q % 2, cols(c)], start=True, stop=True)
                    mm.then_inc(s["kq_p"], 1)
                if slot == 10:
                    pe.wait_ge(s["PT_ready"], n + 1)
                    for c in range(NC):
                        mm = pe.transpose(PA[1][:, cols(c)], kT[:, q, cols(c)], ident)
                    mm.then_inc(s["ktm_p"], 1)
                if slot == 12:
                    pe.wait_ge(s["kd_ready"], n + 1)
                    for c in range(NC):
                        mm = pe.transpose(PA[1][:, cols(c)], vT[:, q % 2, cols(c)], ident)
                    mm.then_inc(s["vtm_p"], 1)

            def invert_part(slot, n, q, j):
                L = len(LEVELS)
                if slot == 0:
                    pe.wait_ge(s["r0_ready"], n + 1)
                    for c in range(NC):
                        mm = pe.transpose(PT_[:, cols(c)], R0[:, q % 2, c], ident)
                    mm.then_inc(s["t0_p"], 1)
                elif slot % 2 == 1:
                    l = slot // 2
                    if l == 0:
                        pe.wait_ge(t0_ready, n + 1)
                    else:
                        pe.wait_ge(t_ready, n * (L - 1) + l)
                    if l == L - 1:
                        pe.sem_inc(passed, 1)
                    for c in range(NC):
                        if l < L - 1:
                            mm = pe.matmul(PY[:, cols(c)], Bt[:, q % 2, c], T[:, c], start=True, stop=True)
                        else:
                            mm = pe.matmul(PY[H:, c * D:c * D + H], Bt[0:H, q % 2, c, H:], T[0:H, c, 0:H],
                                           start=True, stop=True)
                    mm.then_inc(y_p, 1)
                    if 0 < l < L - 1:
                        if l == 1 and not (isinstance(n, int) and n == 0):
                            pe.wait_ge(r_ready, n * L)
                        for c in range(NC):
                            mm = pe.transpose(PR[:, cols(c)], T[:, c], ident)
                        mm.then_inc(r_p, 1)
                else:
                    l = slot // 2 - 1
                    if l:
                        pe.wait_ge(r_ready, n * L + l)
                    pe.wait_ge(ym_ready, n * L + l + 1)
                    if l >= L - 2:
                        pe.sem_inc(passed, 1)
                    R = R0[:, q % 2] if l == 0 else Rl[:, (l - 1) % 2]
                    if l < L - 1:
                        for c in range(NC):
                            if l < L - 2:
                                mm = pe.matmul(PT_[:, cols(c)], R[:, c], Ym[:, c], start=True, stop=True)
                            else:
                                mm = pe.matmul(PT_[0:H, c * D:c * D + H], R[0:H, c, 0:H], Ym[0:H, c, 0:H],
                                               start=True, stop=True)
                        mm.then_inc(t_p, 1)
                    if l == L - 2:
                        for c in range(NC):
                            mm = pe.matmul(PR[:, cols(c)], Ym[:, c], R[:, c], start=True, stop=True)
                        mm.then_inc(r_p, 1)
                    if l == L - 1:
                        for c in range(NC):
                            mm = pe.matmul(PR[0:H, c * D + H:c * D + D], Ym[H:, c, 0:H], Rf[H:, q % 2, c, H:],
                                           start=True, stop=True)
                        mm.then_inc(r_p, 1)

            def scan_part(slot, n, q, j):
                if slot >= 3 * NC:
                    return
                c, phase = divmod(slot, 3)
                o = CO[:, c * D:c * D + D]
                tok = slice(c * D, c * D + D)
                if phase == 0 and c:
                    pe.wait_ge(s_ready, n * (NC - 1) + c)
                    pe.matmul(KS, kT[:, q, tok], S[:, :], start=True, stop=True).then_inc(ks_p, 1)
                    pe.matmul(o, qg[:, q, tok], S[:, :], start=True, stop=False)
                if phase == 1:
                    if c:
                        pe.wait_ge(w_ready, n * (NC - 1) + c)
                    else:
                        pe.wait_ge(r_ready, n * len(LEVELS) + len(LEVELS))
                    pe.matmul(US, Rf[:, q % 2, c], W[:, :] if c else Vn[:, q, 0], start=True, stop=True).then_inc(u_p, 1)
                if phase == 2:
                    pe.wait_ge(u_ready, n * NC + c + 1)
                    if c < NC - 1:
                        pe.matmul(SS, Kd[:, q, c], U[:, :], start=True, stop=True).then_inc(s_p, 1)
                    if c == 0:
                        wait_prior("O_ready", n)
                    mm = pe.matmul(o, PT[:, q, c], U[:, :], start=(c == 0), stop=True)
                    if c == NC - 1:
                        mm.then_inc(s_p, 1)

            def finish_part(slot, n, q, j):
                p = q % 2
                if slot == 4:
                    pe.wait_ge(s["on_ready"], n + 1)
                    wait_prior("lg_ready", n)
                    for c in range(NC):
                        mm = pe.transpose(PD[:, c * D:c * D + D], on[:, c], ident)
                    mm.then_inc(s["on_tp"], 1)
                if slot == 5:
                    pe.wait_ge(s["onT_ready"], n + 1)
                    for c in range(NC):
                        mm = pe.matmul(PD[:, c * D:c * D + D], onT[:, c * D:c * D + D], wo[:, :], start=True, stop=True)
                    mm.then_inc(s["oproj_p"], 1)
                if slot == 11:
                    pe.wait_ge(s["x2_ready"], n + 1)
                    for c in range(NC):
                        mm = pe.transpose(PD[:, c * D:c * D + D], x2[:, c], ident)
                    mm.then_inc(s["x2_tp"], 1)
                if slot == 12:
                    pe.wait_ge(s["x2T_ready"], n + 1)
                    pe.matmul(PD[0:EXPERTS, :], w[:, W_GATE:W_GATE + EXPERTS], x2T[:, p], start=True, stop=True
                              ).then_inc(s["logit_p"], 1)

            pe.wait_ge(wo_ready, 1)

            def iteration(gather, project, product, invert, scan, finish):
                for slot in range(SLOTS):
                    if invert:
                        invert_part(slot, *invert)
                    if scan:
                        scan_part(slot, *scan)
                    if project:
                        project_part(slot, *project)
                    if product:
                        product_part(slot, *product)
                    if finish:
                        finish_part(slot, *finish)
                    if gather:
                        gather_part(slot, *gather)

            pipeline(pe, iteration)

            for h in range(2):
                pe.wait_ge(sk[h], 4)
                for c in range(NC):
                    mm = pe.transpose(bank[4 + h][:, cols(c)], K2[:, h, cols(c)], ident)
                mm.then_inc(kt_p[h], 1)
            for it in range(SINKHORN - 1):
                for h in range(2):
                    pe.wait_ge(sk[h], 5 + 4 * it + 2)
                    for c in range(NC):
                        mm = pe.matmul(bank[h][:, c * HALF:c * HALF + HALF], K2[:, h, cols(c)], c16[:, h],
                                       start=True, stop=True)
                    mm.then_inc(rows_p[h], 1)
                for h in range(2):
                    if it == 0:
                        pe.wait_ge(kt_ready[h], 1)
                    pe.wait_ge(sk[h], 5 + 4 * it + 3)
                    for c in range(NC):
                        mm = pe.matmul(bank[2 + h][:, 0:HALF], K2T[:, h, c], r_tok[:, h, c * HALF:c * HALF + HALF],
                                       start=(c == 0), stop=(c == NC - 1))
                    mm.then_inc(cols_p[h], 1)
            for h in range(2):
                pe.wait_ge(sk[h], 5 + 4 * (SINKHORN - 1) + 2)
                pe.matmul(bank[h][:, :], blockc[:, h], K2[:, h], start=True, stop=True).then_inc(rows_p[h], 1)
            DONE = 5 + 4 * SINKHORN
            for h in range(2):
                pe.wait_ge(sk[h], DONE + 2 * (TOP // 8) + 1)
                pe.matmul(bank[h][:, :], cst[:, C_HIGHER:C_HIGHER + D], r2[:, h], start=True, stop=True
                          ).then_inc(higher_p[h], 1)
            for h in range(2):
                pe.wait_ge(sk[h], DONE + 2 * (TOP // 8) + 3)
                for c in range(NC):
                    mm = pe.transpose(bank[2 + h][:, c * D:c * D + D], work2[:, h, c * D:c * D + D], ident)
                mm.then_inc(wt_p[h], 1)
            pe.wait_ge(wt_ready, 2)

            def experts(n, q, j):
                pe.wait_ge(batch_in[q], 16 * (j + 1))
                for c in range(NC):
                    if c % 2 == 0 and not (isinstance(n, int) and n == 0):
                        pe.wait_ge(acc_e[3], n * 2 - 1 + c // 2)
                        pe.wait_ge(part_ready, n * 2 - 1 + c // 2)
                    for k in range(2):
                        mm = pe.matmul(bank[2 * c + k][:, :], xb[:, q, c * D:c * D + D],
                                       w[:, W_EXP + PE_BANK * k:W_EXP + PE_BANK * (k + 1)], start=True, stop=True)
                    mm.then_inc(y_chunk, 1)

            sequences(pe, experts)

        @block.scalar
        def _(act):
            act.wait_ge(w_in, 16)
            act.activation(neg_a[:, :], w[:, W_ALOG:W_ALOG + 1], ACT.Exp).then_inc(a_exp, 1)

            def gather_part(slot, n, q, j):
                if slot == 11:
                    act.wait_ge(s["x_tp"], n + 1)
                    act.activation(xT[:, :], PA[0][:, :], ACT.Copy).then_inc(s["xT_ready"], 1)

            def project_part(slot, n, q, j):
                for t, at, k in (("q", 0, 0), ("k", 3, 1), ("v", 6, 2)):
                    if slot == at:
                        act.wait_ge(proj_p[t], n + 1)
                        act.activation(conv[t][:, :], PA[0][:, :], ACT.Copy,
                                       scale=w[:, W_CONV + TAPS * k + TAPS - 1:W_CONV + TAPS * k + TAPS]
                                       ).then_inc(tap[t][0], 1)
                for t, at, dst in (("q", 4, qT[:, q % 2]), ("k", 5, kT[:, q]), ("v", 9, vT[:, q % 2])):
                    if slot == at:
                        act.wait_ge(tap[t][TAPS - 1], n + 1)
                        if t == "q" and not (isinstance(n, int) and n < 2):
                            act.wait_ge(s["qg_ready"], n - 1)
                        act.activation(dst, conv[t][:, :], ACT.Silu).then_inc(silu[t], 1)
                if slot == 10:
                    act.wait_ge(s["gate_p"], n + 1)
                    act.wait_ge(s["ab_sb"], n + 1)
                    if not (isinstance(n, int) and n < RING):
                        act.wait_ge(s["on_ready"], n - RING + 1)
                    act.activation(gate[:, q, 0:NC - 1],
                                   PA[0][:, 0:(NC - 1) * GATE].rearrange("p (c x) -> p c x", x=GATE)[:, :, 0:D], ACT.Silu)
                    act.activation(gate[:, q, NC - 1], PM[:, 0:D], ACT.Silu).then_inc(s["gate_ready"], 1)
                    act.preload_act_table_set("natural_log_exp_and_others")
                if slot == 11:
                    act.activation(eb[:, :], ab[:, 1], ACT.Exp, scale=-1.0).then_inc(s["beta_e"], 1)
                    act.wait_ge(s["zabs_ready"], n + 1)
                    act.activation(ez[:, :], zabs[:, :], ACT.Exp, scale=-1.0).then_inc(s["z_exp"], 1)
                    act.wait_ge(s["z_exp"], n + 1)
                    act.activation(lz[:, :], ez[:, :], ACT.Ln, bias=1.0).then_inc(s["z_log"], 1)

            def product_part(slot, n, q, j):
                if slot == 2:
                    act.wait_ge(s["G_ready"], n + 1)
                    act.activation(gam_tok[:, q], G[:, :], ACT.Exp).then_inc(s["gam_tok_ready"], 1)
                    act.wait_ge(s["gdiff_ready"], n + 1)
                    act.activation(gexp[:, :], gdiff[:, :], ACT.Exp).then_inc(s["gexp_ready"], 1)
                    act.wait_ge(s["earg_ready"], n + 1)
                    act.wait_ge(s["Gbc_p"], n + 1)
                    if not (isinstance(n, int) and n == 0):
                        act.wait_ge(s["qg_ready"], n)
                    act.activation(gam[:, :, :], chunks(PA[1][:, :]), ACT.Exp).then_inc(s["gam_ready"], 1)
                    act.activation(E[:, :, :], earg[:, :, :], ACT.Exp).then_inc(s["E_ready"], 1)

            def invert_part(slot, n, q, j):
                L = len(LEVELS)
                if slot % 2 == 0 and slot:
                    l = slot // 2 - 1
                    if l < L - 1:
                        act.wait_ge(t_p, n * (L - 1) + l + 1)
                        if l < L - 2:
                            a = act.activation(T[:, :, :], chunks(PT_[:, :]), ACT.Copy)
                        else:
                            a = act.activation(T[0:H, :, 0:H], chunks(PT_[0:H, :])[:, :, 0:H], ACT.Copy)
                        a.then_inc(t_ready, 1)
                    if l >= L - 2:
                        act.wait_ge(r_p, n * L + l + 1)
                        if l == L - 2:
                            a = act.activation(Rf[:, q % 2], chunks(PR[:, :]), ACT.Copy)
                        else:
                            a = act.activation(Rf[0:H, q % 2, :, H:], chunks(PR[0:H, :])[:, :, H:], ACT.Copy)
                        a.then_inc(r_ready, 1)
                elif 3 <= slot < 2 * L - 1:
                    l = slot // 2 - 1
                    act.wait_ge(r_p, n * L + l + 1)
                    act.activation(Rl[:, l % 2], chunks(PR[:, :]), ACT.Copy).then_inc(r_ready, 1)

            def scan_part(slot, n, q, j):
                c, phase = divmod(slot, 3)
                if c < NC and phase == 1:
                    act.wait_ge(u_p, n * NC + c + 1)
                    act.activation(U[:, :], US, ACT.Copy).then_inc(u_ready, 1)
                if slot == SLOTS - 1:
                    act.wait_ge(s_p, n * NC + NC)
                    act.activation(O[:, q % 2], chunks(CO[:, :]), ACT.Copy).then_inc(s["O_ready"], 1)

            def finish_part(slot, n, q, j):
                p = q % 2
                if slot == 1:
                    act.wait_ge(s["O_ready"], n + 1)
                    for c in range(NC):
                        a = act.activation(junk[:, c], O[:, p, c], ACT.Square, accum_out=so[:, c:c + 1])
                    a.then_inc(s["o_sq"], 1)
                if slot == 4:
                    act.wait_ge(s["on_tp"], n + 1)
                    act.activation(onT[:, :], PD[:, :], ACT.Copy).then_inc(s["onT_ready"], 1)
                if slot == 11:
                    act.wait_ge(s["x2_tp"], n + 1)
                    if not (isinstance(n, int) and n < 2):
                        act.wait_ge(x2_stored[p], 16 * (j * 2 + q // 2))
                    act.activation(x2T[:, p], PD[:, :], ACT.Copy).then_inc(s["x2T_ready"], 1)
                if slot == 12:
                    act.wait_ge(s["logit_p"], n + 1)
                    if not (isinstance(n, int) and n < 2):
                        act.wait_ge(lg_stored[p], 16 * (j * 2 + q // 2))
                    act.activation(lg[:, p], PD[0:EXPERTS, :], ACT.Copy).then_inc(s["lg_ready"], 1)

            def iteration(gather, project, product, invert, scan, finish):
                for slot in range(SLOTS):
                    if invert:
                        invert_part(slot, *invert)
                    if scan:
                        scan_part(slot, *scan)
                    if product:
                        product_part(slot, *product)
                    if finish:
                        finish_part(slot, *finish)
                    if project:
                        project_part(slot, *project)
                    if gather:
                        gather_part(slot, *gather)

            pipeline(act, iteration)

            for h in range(2):
                act.wait_ge(kt_p[h], 1)
                act.activation(K2T[:, h], chunks(bank[4 + h][:, :]), ACT.Copy).then_inc(kt_ready[h], 1)

            def scale(n, q, j):
                p = q % 2
                act.wait_ge(gcur_ready, n + 1)
                if not (isinstance(n, int) and n < 2):
                    act.wait_ge(sum_ab, n - 1)
                for c in range(NC):
                    act.wait_ge(y_chunk, n * NC + c + 1)
                    for e in range(4):
                        a = act.activation(part[p][:, e, c], bank[2 * c + 1][:, e * D:e * D + D], ACT.Copy,
                                           scale=gcur[:, p, c, 4 + e:5 + e])
                    if c % 2:
                        a.then_inc(part_ready, 1)

            sequences(act, scale)

        @block.vector
        def _(dve):
            dve.wait_ge(w_in, 16)
            dve.tensor_scalar(wo[:, :], w[:, W_O:W_O + D], w[:, W_NORM:W_NORM + 1], None, ALU.mult).then_inc(wo_ready, 1)
            dve.wait_ge(a_exp, 1)
            dve.tensor_scalar(neg_a[:, :], neg_a[:, :], -1.0, None, ALU.mult).then_inc(neg_a_ready, 1)
            dve.wait_ge(neg_a_ready, 1)
            dve.wait_ge(cst_in, 16)

            def norm_stats(src, st, mv, ve, n, stats, aggr, var):
                for c in range(NC):
                    a = dve.bn_stats(st[:, c, :], src[:, c])
                a.then_inc(stats, 1)
                dve.wait_ge(stats, n + 1)
                dve.sem_inc(passed, 1)
                for c in range(NC):
                    a = dve.bn_aggr(mv[:, c, :], st[:, c, :])
                a.then_inc(aggr, 1)
                dve.wait_ge(aggr, n + 1)
                dve.tensor_scalar(ve[:, :], mv[:, :, 1], 1e-5, None, ALU.add).then_inc(var, 1)

            def normalize(src, mv, rs, dst, n, rstd_, ready):
                dve.wait_ge(rstd_, n + 1)
                for c in range(NC):
                    a = dve.tensor_scalar(dst[:, c, :], src[:, c], mv[:, c, 0:1], rs[:, c:c + 1],
                                          ALU.subtract, ALU.mult)
                a.then_inc(ready, 1)

            def taps(t, k, n, which):
                for i in which:
                    dve.wait_ge(tap[t][i - 1], n + 1)
                    at = W_CONV + TAPS * k + TAPS - 1 - i
                    dve.scalar_tensor_tensor(out=conv[t][:, i:], in0=PA[0][:, 0:TOKENS - i], scalar=w[:, at:at + 1],
                                             in1=conv[t][:, i:], op0=ALU.mult, op1=ALU.add).then_inc(tap[t][i], 1)

            def gather_part(slot, n, q, j):
                if slot == 5:
                    dve.wait_ge(gathered[q % 2], 16 * NC * uses(q, j))
                    norm_stats(h_in[:, q % 2], st1, mv1, ve1, n, s["ln_stats"], s["ln_aggr"], s["ln_var"])

            def project_part(slot, n, q, j):
                if slot == 1:
                    taps("q", 0, n, (1, 2))
                if slot == 2:
                    taps("q", 0, n, (3,))
                if slot == 3:
                    taps("k", 1, n, (1, 2))
                if slot == 4:
                    taps("k", 1, n, (3,))
                if slot == 7:
                    taps("v", 2, n, (1, 2))
                if slot == 8:
                    taps("v", 2, n, (3,))
                if slot == 9:
                    dve.wait_ge(s["gate_p"], n + 1)
                    dve.tensor_copy(ab[:, :, 0:NC - 1],
                                    PA[0][:, 0:(NC - 1) * GATE].rearrange("p (c x) -> p x c", x=GATE)[:, D:, :])
                    dve.tensor_copy(ab[:, :, NC - 1], PM[:, D:GATE]).then_inc(s["ab_sb"], 1)
                    dve.wait_ge(s["ab_sb"], n + 1)
                    dve.tensor_scalar(z[:, :], ab[:, 0], w[:, W_DT:W_DT + 1], None, ALU.add).then_inc(s["z_ready"], 1)
                    dve.wait_ge(s["z_ready"], n + 1)
                    dve.scalar_tensor_tensor(out=zabs[:, :], in0=z[:, :], scalar=-1.0, in1=z[:, :], op0=ALU.mult,
                                             op1=ALU.max).then_inc(s["zabs_ready"], 1)
                if slot == 12:
                    dve.wait_ge(s["z_log"], n + 1)
                    dve.scalar_tensor_tensor(out=sp[:, :], in0=z[:, :], scalar=0.0, in1=lz[:, :],
                                             op0=ALU.max, op1=ALU.add).then_inc(s["soft_ready"], 1)
                    dve.tensor_scalar(beta1[:, :], eb[:, :], 1.0, None, ALU.add).then_inc(s["beta_one"], 1)
                    dve.wait_ge(s["soft_ready"], n + 1)
                    dve.tensor_scalar(g[:, :], sp[:, :], neg_a[:, 0:1], None, ALU.mult).then_inc(s["g_ready"], 1)
                    dve.wait_ge(s["beta_one"], n + 1)
                    dve.reciprocal(beta[:, :], beta1[:, :]).then_inc(s["beta_ready"], 1)

            def product_part(slot, n, q, j):
                if slot == 0:
                    dve.wait_ge(s["G_p"], n + 1)
                    dve.tensor_copy(G[:, :], G_P).then_inc(s["G_ready"], 1)
                if slot == 2:
                    dve.wait_ge(s["Gbc_p"], n + 1)
                    dve.wait_ge(s["G_ready"], n + 1)
                    dve.tensor_tensor(gdiff[:, :], chunks(PA[1][:, :])[:, :, D - 1], G[:, :], ALU.subtract
                                      ).then_inc(s["gdiff_ready"], 1)
                    for c in range(NC):
                        a = dve.scalar_tensor_tensor(out=earg[:, c], in0=PA[1][:, c * D:c * D + D],
                                                     scalar=G[:, c:c + 1], in1=below, op0=ALU.subtract, op1=ALU.min)
                    a.then_inc(s["earg_ready"], 1)
                if slot == 4:
                    dve.wait_ge(s["kk_p"], n + 1)
                    for c in range(NC):
                        a = dve.tensor_tensor_reduce(Braw[:, c], PA[1][:, c * D:c * D + D], ident, 1.0, 0.0,
                                                     ALU.mult, ALU.add, ssk[:, c:c + 1])
                    a.then_inc(s["ssk_ready"], 1)
                    dve.wait_ge(s["ssk_ready"], n + 1)
                    dve.tensor_scalar(ss[:, :], ssk[:, :], 1e-6, None, ALU.add).then_inc(s["ss_ready"], 1)
                    dve.wait_ge(s["ss_ready"], n + 1)
                    dve.reciprocal(rk[:, :], ss[:, :]).then_inc(s["rk_ready"], 1)
                    dve.wait_ge(s["gam_ready"], n + 1)
                    dve.tensor_copy(gam_end[:, q], gam[:, :, D - 1])
                    dve.wait_ge(s["rk_ready"], n + 1)
                    dve.wait_ge(s["beta_ready"], n + 1)
                    dve.tensor_tensor(cj[:, :], rk[:, :], beta[:, :], ALU.mult).then_inc(s["cj_ready"], 1)
                if slot == 5:
                    dve.wait_ge(s["cj_ready"], n + 1)
                    dve.wait_ge(s["E_ready"], n + 1)
                    for c in range(NC):
                        a = dve.scalar_tensor_tensor(out=Braw[:, c], in0=PA[1][:, c * D:c * D + D],
                                                     scalar=cj[:, c:c + 1], in1=E[:, c], op0=ALU.mult, op1=ALU.mult)
                    a.then_inc(s["braw_ready"], 1)
                if slot == 6:
                    dve.wait_ge(s["gexp_ready"], n + 1)
                    dve.tensor_tensor(kdec[:, :], gexp[:, :], cj[:, :], ALU.mult).then_inc(s["kdec_ready"], 1)
                if slot == 8:
                    dve.wait_ge(s["sums_p"], n + 1)
                    dve.tensor_scalar(eps_q[:, q], SS_P, 1e-6, 1e-5 * D, ALU.add, ALU.mult).then_inc(s["epsq_ready"], 1)
                if slot == 9:
                    dve.wait_ge(s["kq_p"], n + 1)
                    dve.wait_ge(s["Ec_ready"], n + 1)
                    dve.tensor_tensor(PT[:, q], chunks(PA[1][:, :]), Ec[:, :, :], ALU.mult).then_inc(s["PT_ready"], 1)
                    dve.wait_ge(s["rss_ready"], n + 1)
                    dve.tensor_tensor(knorm[:, :], ss[:, :], rss[:, :], ALU.mult).then_inc(s["knorm_ready"], 1)
                if slot == 11:
                    dve.wait_ge(s["ktm_p"], n + 1)
                    dve.wait_ge(s["kdec_ready"], n + 1)
                    dve.tensor_tensor(Kd[:, q], chunks(PA[1][:, :]), kdec[:, :].unsqueeze(2).broadcast_to([D, NC, D]),
                                      ALU.mult).then_inc(s["kd_ready"], 1)
                if slot == 12:
                    dve.wait_ge(s["vtm_p"], n + 1)
                    dve.wait_ge(s["knorm_ready"], n + 1)
                    dve.tensor_tensor(Vn[:, q], chunks(PA[1][:, :]), knorm[:, :].unsqueeze(2).broadcast_to([D, NC, D]),
                                      ALU.mult).then_inc(s["vn_ready"], 1)

            def invert_part(slot, n, q, j):
                L = len(LEVELS)
                if slot == 0:
                    dve.wait_ge(s["t0_p"], n + 1)
                    dve.tensor_copy(T[:, :, :], chunks(PT_[:, :])).then_inc(t0_ready, 1)
                if slot % 2 == 1:
                    l = slot // 2
                    dve.wait_ge(y_p, n * L + l + 1)
                    if l < L - 1:
                        at = C_LEVEL + l * D
                        a = dve.tensor_tensor(Ym[:, :, :], chunks(PY[:, :]),
                                              cst[:, at:at + D].unsqueeze(1).broadcast_to([D, NC, D]), ALU.mult)
                    else:
                        a = dve.tensor_scalar(Ym[H:, :, 0:H], chunks(PY[H:, :])[:, :, 0:H], -1.0, None, ALU.mult)
                    a.then_inc(ym_ready, 1)

            def scan_part(slot, n, q, j):
                if slot >= 3 * NC:
                    return
                c, phase = divmod(slot, 3)
                if phase == 0 and c:
                    dve.wait_ge(ks_p, n * (NC - 1) + c)
                    dve.scalar_tensor_tensor(out=W[:, :], in0=KS, scalar=gam_tok[:, q, c:c + 1], in1=Vn[:, q, c],
                                             op0=ALU.mult, op1=ALU.subtract, reverse1=True).then_inc(w_ready, 1)
                if phase == 2 and c < NC - 1:
                    dve.wait_ge(s_p, n * NC + c + 1)
                    if c == 0:
                        dve.tensor_copy(S[:, :], SS).then_inc(s_ready, 1)
                    else:
                        dve.wait_ge(s_ready, n * (NC - 1) + c)
                        dve.scalar_tensor_tensor(out=S[:, :], in0=S[:, :], scalar=gam_end[:, q, c:c + 1], in1=SS,
                                                 op0=ALU.mult, op1=ALU.add).then_inc(s_ready, 1)

            def finish_part(slot, n, q, j):
                p = q % 2
                if slot == 2:
                    dve.wait_ge(s["o_sq"], n + 1)
                    dve.scalar_tensor_tensor(out=ms1[:, :], in0=so[:, :], scalar=1.0 / D, in1=eps_q[:, q],
                                             op0=ALU.mult, op1=ALU.add).then_inc(s["ms1_ready"], 1)
                if slot == 3:
                    dve.wait_ge(s["rstd_ready"], n + 1)
                    for c in range(NC):
                        a = dve.scalar_tensor_tensor(out=on[:, c], in0=O[:, p, c], scalar=rstd[:, c:c + 1],
                                                     in1=gate[:, q, c], op0=ALU.mult, op1=ALU.mult)
                    a.then_inc(s["on_ready"], 1)
                h = hall[:, bass.ds(n, 1)].rearrange("p a c d -> p (a c) d")
                if slot == 6:
                    dve.wait_ge(s["oproj_p"], n + 1)
                    dve.wait_ge(hall_in[p], 16 * uses(q, j))
                    dve.tensor_tensor(h, chunks(PD[:, :]), h, ALU.add).then_inc(s["h2_ready"], 1)
                if slot == 7:
                    dve.wait_ge(s["h2_ready"], n + 1)
                    dve.sem_inc(passed, 1)
                    norm_stats(h, st2, mv2, ve2, n, s["ln2_stats"], s["ln2_aggr"], s["ln2_var"])
                if slot == 9:
                    normalize(h, mv2, rs2, x2, n, s["ln2_rstd"], s["x2_ready"])

            def iteration(gather, project, product, invert, scan, finish):
                for slot in range(SLOTS):
                    if invert:
                        invert_part(slot, *invert)
                    if scan:
                        scan_part(slot, *scan)
                    if product:
                        product_part(slot, *product)
                    if finish:
                        finish_part(slot, *finish)
                    if project:
                        project_part(slot, *project)
                    if gather:
                        gather_part(slot, *gather)

            pipeline(dve, iteration)

            count = [0, 0]

            def link(h, ins):
                count[h] += 1
                ins.then_inc(sk[h], 1)

            def after(h):
                dve.wait_ge(sk[h], count[h])

            for h in range(2):
                dve.wait_ge(k_in[h], 16)
                link(h, dve.tensor_scalar(K2[:, h], K2[:, h], 1e-6, None, ALU.max))
            for h in range(2):
                after(h)
                link(h, dve.tensor_reduce(col2[:, h, 0:1], K2[:, h], AX.X, ALU.max))
            for h in range(2):
                after(h)
                link(h, dve.reciprocal(col2[:, h, 1:2], col2[:, h, 0:1]))
            for h in range(2):
                after(h)
                link(h, dve.tensor_scalar(K2[:, h], K2[:, h], col2[:, h, 1:2], None, ALU.mult))
            for h in range(2):
                after(h)
                link(h, dve.tensor_reduce(col2[:, h, 2:3], K2[:, h], AX.X, ALU.add))
            for it in range(SINKHORN):
                for h in range(2):
                    after(h)
                    link(h, dve.reciprocal(col2[:, h, 3:4], col2[:, h, 2:3]))
                if it < SINKHORN - 1:
                    for h in range(2):
                        after(h)
                        link(h, dve.tensor_scalar(c16[:, h], owner, col2[:, h, 3:4], None, ALU.mult))
                    for h in range(2):
                        dve.wait_ge(rows_p[h], it + 1)
                        link(h, dve.reciprocal(r_tok[:, h], bank[h][:, 0:NC * HALF]))
                    for h in range(2):
                        dve.wait_ge(cols_p[h], it + 1)
                        link(h, dve.tensor_tensor_reduce(own[:, h], bank[2 + h][:, 0:HALF], owner, 1.0, 0.0,
                                                         ALU.mult, ALU.add, col2[:, h, 2:3]))
                else:
                    for h in range(2):
                        after(h)
                        link(h, dve.tensor_scalar(blockc[:, h], cst[:, C_BLOCK:C_BLOCK + D], col2[:, h, 3:4], None,
                                                  ALU.mult))
                    for h in range(2):
                        dve.wait_ge(rows_p[h], it + 1)
                        link(h, dve.reciprocal(r2[:, h], bank[h][:, :]))
                    for h in range(2):
                        after(h)
                        link(h, dve.scalar_tensor_tensor(out=gates2[:, h], in0=K2[:, h], scalar=col2[:, h, 3:4],
                                                         in1=r2[:, h], op0=ALU.mult, op1=ALU.mult))
            for k in range(TOP // 8):
                src = work2 if k else gates2
                for h in range(2):
                    after(h)
                    link(h, dve.max(top8[:, h], src[:, h]))
                for h in range(2):
                    after(h)
                    link(h, dve.match_replace(work2[:, h], top8[:, h], src[:, h], -1.0))
            for h in range(2):
                after(h)
                link(h, dve.tensor_scalar(r2[:, h], work2[:, h], 0.0, None, ALU.is_lt))
            for h in range(2):
                after(h)
                link(h, dve.tensor_tensor(prod2[:, h], gates2[:, h], r2[:, h], ALU.mult))
            for h in range(2):
                after(h)
                dve.wait_ge(higher_p[h], 1)
                link(h, dve.scalar_tensor_tensor(out=work2[:, h], in0=bank[h][:, :], scalar=0.5, in1=prod2[:, h],
                                                 op0=ALU.is_lt, op1=ALU.mult))
            for h in range(2):
                dve.wait_ge(wt_p[h], 1)
                for c in range(NC):
                    a = dve.tensor_copy(wt[:, HALF * h:HALF * h + HALF, c, :],
                                        bank[2 + h][:, c * D:c * D + D].rearrange("p (b e) -> p b e", e=EXPERTS))
                a.then_inc(wt_ready, 1)
            dve.wait_ge(wt_ready, 2)

            def combine(n, q, j):
                p = q % 2
                if not (isinstance(n, int) and n < 2):
                    dve.wait_ge(part_ready, n * 2 - 2)
                    dve.wait_ge(out_ready, n - 1)
                dve.tensor_copy(gcur[:, p], wt[:, bass.ds(n, 1)].rearrange("p a c e -> p (a c) e")
                                ).then_inc(gcur_ready, 1)
                dve.wait_ge(gcur_ready, n + 1)
                for pair in range(NC // 2):
                    dve.wait_ge(y_chunk, n * NC + 2 * pair + 2)
                    for e in range(4):
                        if e:
                            dve.wait_ge(acc_e[e - 1], n * 2 + pair + 1)
                        for c in (2 * pair, 2 * pair + 1):
                            a = dve.scalar_tensor_tensor(out=acc[:, p, c], in0=bank[2 * c][:, e * D:e * D + D],
                                                         scalar=gcur[:, p, c, e:e + 1],
                                                         in1=acc[:, p, c] if e else hall[:, bass.ds(n, 1), c].rearrange("p a d -> p (a d)"),
                                                         op0=ALU.mult, op1=ALU.add)
                        a.then_inc(acc_e[e], 1)

            sequences(dve, combine)


def kernel(**inputs):
    import numpy as _np
    import concourse.bacc as _bacc
    from concourse import mybir as _mybir
    from concourse.bass_utils import run_bass_kernel_spmd as _run

    x = _np.asarray(inputs["x"])
    a = {k: _np.asarray(v) for k, v in inputs.items()}
    ids = _np.ascontiguousarray(x.reshape(SEQS * NC, CHUNK).T)
    packed = _np.concatenate(
        [a[f"L0_attn_{k}_proj_w"].T for k in "qkvog"]
        + [a["L0_attn_a_proj_w"].T, a["L0_attn_b_proj_w"].T]
        + [a[f"L0_attn_{k}_conv_w"] for k in "qkv"]
        + [a["L0_attn_o_norm_w"].reshape(D, 1)]
        + [_np.broadcast_to(a["L0_attn_A_log"].reshape(1, 1), (D, 1)),
           _np.broadcast_to(a["L0_attn_dt_bias"].reshape(1, 1), (D, 1))]
        + [a["L0_ffn_gate_weight"].reshape(D, EXPERTS)]
        + [a["L0_ffn_experts"].transpose(1, 0, 2).reshape(D, EXPERTS * D)], axis=1)
    arrays = {
        "ids_dram": ids,
        "table_dram": _np.ascontiguousarray(a["L0_tok_idx2vec"]),
        "weights_dram": _np.ascontiguousarray(packed),
        "consts_dram": shape_constants(),
    }
    nc = _bacc.Bacc("TRN2", target_bir_lowering=False, num_devices=1)
    args = [nc.dram_tensor(k, v.shape, _mybir.dt.from_np(v.dtype), kind="ExternalInput").ap() for k, v in arrays.items()]
    f32 = _mybir.dt.float32
    out = nc.dram_tensor("out_dram", (SEQS, TOKENS, D), f32, kind="ExternalOutput").ap()
    x2 = nc.dram_tensor("x2_dram", (SEQS, D, TOKENS), f32, kind="Internal").ap()
    logit = nc.dram_tensor("logit_dram", (SEQS * EXPERTS, TOKENS), f32, kind="Internal").ap()
    tower(nc, *args, out, x2, logit)
    r = _run(nc, [arrays], core_ids=[0])
    return r.results[0]["out_dram"]
```
